# Optimizing a Trainium2 kernel written in Bass

```python
import numpy as np
import jax
import jax.numpy as jnp

def _softmax(x, axis=-1):
    return jax.nn.softmax(x, axis=axis)

def _gelu(x):
    return jax.nn.gelu(x, approximate=True)

def _silu(x):
    return jax.nn.silu(x)

def _sigmoid(x):
    return jax.nn.sigmoid(x)

def _layernorm(x, axis=-1, eps=1e-05):
    m = jnp.mean(x, axis=axis, keepdims=True)
    v = jnp.var(x, axis=axis, keepdims=True)
    return (x - m) / jnp.sqrt(v + eps)

def _scatter_add(tgt, idx, src, axis=0):
    return tgt.at[idx].add(src)

def _segment_sum(src, seg, n):
    return jax.ops.segment_sum(src, seg, n)
kernel_name = 'mk_conv_preact_d2_conv_nchw256_r2_c597e8'

def setup_inputs(seed: int=0):
    np.random.seed(seed)
    _w = jnp.asarray

    def _rec_inputs():
        import jax
        import jax.numpy as jnp
        _gk = jax.random.key(seed)
        x = -8.268e-05 + 0.9999 * jax.random.normal(jax.random.fold_in(_gk, 1), (4, 128, 112, 112), jnp.float32)
        return x
    x = _rec_inputs()

    def _L0_conv_setup():
        import jax, jax.numpy as jnp
        import numpy as np
        WIN = 8
        HEADS = 8
        LN_EPS = 1e-05
        key = jax.random.key(seed)
        ks = jax.random.split(key, 4)
        B, C, H, W = (4, 128, 112, 112)
        x = jax.random.normal(ks[0], (B, C, H, W), jnp.float32)
        ln_gamma = jnp.ones((C,), jnp.float32)
        ln_beta = jnp.zeros((C,), jnp.float32)
        s_in = float(np.sqrt(6.0 / (C + 3 * C)))
        w_qkv = jax.random.uniform(ks[1], (3 * C, C), jnp.float32, -s_in, s_in)
        b_qkv = jnp.zeros((3 * C,), jnp.float32)
        s_out = float(np.sqrt(6.0 / (C + C)))
        w_out = jax.random.uniform(ks[2], (C, C), jnp.float32, -s_out, s_out)
        b_out = jnp.zeros((C,), jnp.float32)
        return {'x': x, 'ln_gamma': ln_gamma, 'ln_beta': ln_beta, 'w_qkv': w_qkv, 'b_qkv': b_qkv, 'w_out': w_out, 'b_out': b_out}
    _L0_conv_all = _L0_conv_setup()
    _L0_conv_in = {k: v for k, v in _L0_conv_all.items() if k in ('ln_gamma', 'ln_beta', 'w_qkv', 'b_qkv', 'w_out', 'b_out')}
    del _L0_conv_all

    def _L1_conv_setup():
        import jax, jax.numpy as jnp
        import numpy as np
        B, C, H, W = (8, 128, 32, 32)
        NH = 8
        CM = 1024
        EPS = 1e-05

        def _repbn(x, g, b, m, v, alpha):
            bn = (x - m) * jax.lax.rsqrt(v + EPS) * g + b
            return bn + alpha * x
        key = jax.random.key(seed)
        ks = jax.random.split(key, 16)
        n = lambda k, s: jax.random.normal(k, s, dtype=jnp.float32) * 0.02
        return {'x': jax.random.normal(ks[0], (B, C, H, W), dtype=jnp.float32), 'Wqkv': n(ks[1], (C, 3 * C)), 'bqkv': n(ks[2], (3 * C,)), 'dw_w': n(ks[3], (C, 1, 3, 3)), 'dw_b': n(ks[4], (C,)), 'Wproj': n(ks[5], (C, C)), 'bproj': n(ks[6], (C,)), 'bn1_g': jnp.ones((C,), jnp.float32), 'bn1_b': jnp.zeros((C,), jnp.float32), 'bn1_m': n(ks[7], (C,)), 'bn1_v': jax.random.uniform(ks[8], (C,), dtype=jnp.float32) + 0.5, 'alpha1': jnp.ones((1,), jnp.float32), 'Wfc1': n(ks[9], (C, CM)), 'bfc1': n(ks[10], (CM,)), 'Wfc2': n(ks[11], (CM, C)), 'bfc2': n(ks[12], (C,)), 'bn2_g': jnp.ones((C,), jnp.float32), 'bn2_b': jnp.zeros((C,), jnp.float32), 'bn2_m': n(ks[13], (C,)), 'bn2_v': jax.random.uniform(ks[14], (C,), dtype=jnp.float32) + 0.5, 'alpha2': jnp.ones((1,), jnp.float32)}
    _L1_conv_all = _L1_conv_setup()
    _L1_conv_in = {k: v for k, v in _L1_conv_all.items() if k in ('Wqkv', 'bqkv', 'dw_w', 'dw_b', 'Wproj', 'bproj', 'bn1_g', 'bn1_b', 'bn1_m', 'bn1_v', 'alpha1', 'Wfc1', 'bfc1', 'Wfc2', 'bfc2', 'bn2_g', 'bn2_b', 'bn2_m', 'bn2_v', 'alpha2')}
    del _L1_conv_all
    return {'x': x, 'L0_conv_ln_gamma': _L0_conv_in['ln_gamma'], 'L0_conv_ln_beta': _L0_conv_in['ln_beta'], 'L0_conv_w_qkv': _L0_conv_in['w_qkv'], 'L0_conv_b_qkv': _L0_conv_in['b_qkv'], 'L0_conv_w_out': _L0_conv_in['w_out'], 'L0_conv_b_out': _L0_conv_in['b_out'], 'L1_conv_Wqkv': _L1_conv_in['Wqkv'], 'L1_conv_bqkv': _L1_conv_in['bqkv'], 'L1_conv_dw_w': _L1_conv_in['dw_w'], 'L1_conv_dw_b': _L1_conv_in['dw_b'], 'L1_conv_Wproj': _L1_conv_in['Wproj'], 'L1_conv_bproj': _L1_conv_in['bproj'], 'L1_conv_bn1_g': _L1_conv_in['bn1_g'], 'L1_conv_bn1_b': _L1_conv_in['bn1_b'], 'L1_conv_bn1_m': _L1_conv_in['bn1_m'], 'L1_conv_bn1_v': _L1_conv_in['bn1_v'], 'L1_conv_alpha1': _L1_conv_in['alpha1'], 'L1_conv_Wfc1': _L1_conv_in['Wfc1'], 'L1_conv_bfc1': _L1_conv_in['bfc1'], 'L1_conv_Wfc2': _L1_conv_in['Wfc2'], 'L1_conv_bfc2': _L1_conv_in['bfc2'], 'L1_conv_bn2_g': _L1_conv_in['bn2_g'], 'L1_conv_bn2_b': _L1_conv_in['bn2_b'], 'L1_conv_bn2_m': _L1_conv_in['bn2_m'], 'L1_conv_bn2_v': _L1_conv_in['bn2_v'], 'L1_conv_alpha2': _L1_conv_in['alpha2']}

def reference(x, L0_conv_ln_gamma, L0_conv_ln_beta, L0_conv_w_qkv, L0_conv_b_qkv, L0_conv_w_out, L0_conv_b_out, L1_conv_Wqkv, L1_conv_bqkv, L1_conv_dw_w, L1_conv_dw_b, L1_conv_Wproj, L1_conv_bproj, L1_conv_bn1_g, L1_conv_bn1_b, L1_conv_bn1_m, L1_conv_bn1_v, L1_conv_alpha1, L1_conv_Wfc1, L1_conv_bfc1, L1_conv_Wfc2, L1_conv_bfc2, L1_conv_bn2_g, L1_conv_bn2_b, L1_conv_bn2_m, L1_conv_bn2_v, L1_conv_alpha2):
    import jax
    import jax.numpy as jnp

    def _L0_conv_ref(x, ln_gamma, ln_beta, w_qkv, b_qkv, w_out, b_out):
        import jax, jax.numpy as jnp
        import numpy as np
        WIN = 8
        HEADS = 8
        LN_EPS = 1e-05
        B, C, H, W = x.shape
        w = WIN
        h = HEADS
        d = C // h
        T = w * w
        xb = jnp.transpose(x, (0, 2, 3, 1))
        win = xb.reshape(B, H // w, w, W // w, w, C)
        win = win.transpose(0, 1, 3, 2, 4, 5).reshape(-1, T, C)
        mu = jnp.mean(win, axis=-1, keepdims=True)
        var = jnp.var(win, axis=-1, keepdims=True)
        xn = (win - mu) * jax.lax.rsqrt(var + LN_EPS) * ln_gamma + ln_beta
        qkv = xn @ w_qkv.T + b_qkv
        q, k, v = jnp.split(qkv, 3, axis=-1)

        def to_heads(t):
            return t.reshape(t.shape[0], T, h, d).transpose(0, 2, 1, 3)
        q, k, v = (to_heads(q), to_heads(k), to_heads(v))
        scale = 1.0 / np.sqrt(d)
        scores = jnp.einsum('nhqd,nhkd->nhqk', q * scale, k)
        attn = jax.nn.softmax(scores, axis=-1)
        o = jnp.einsum('nhqk,nhkd->nhqd', attn, v)
        o = o.transpose(0, 2, 1, 3).reshape(-1, T, C)
        o = o @ w_out.T + b_out
        out = o.reshape(B, H // w, W // w, w, w, C)
        out = out.transpose(0, 1, 3, 2, 4, 5).reshape(B, H, W, C)
        return jnp.transpose(out, (0, 3, 1, 2))

    def _L1_conv_ref(x, Wqkv, bqkv, dw_w, dw_b, Wproj, bproj, bn1_g, bn1_b, bn1_m, bn1_v, alpha1, Wfc1, bfc1, Wfc2, bfc2, bn2_g, bn2_b, bn2_m, bn2_v, alpha2):
        import jax, jax.numpy as jnp
        import numpy as np
        B, C, H, W = (8, 128, 32, 32)
        NH = 8
        CM = 1024
        EPS = 1e-05

        def _repbn(x, g, b, m, v, alpha):
            bn = (x - m) * jax.lax.rsqrt(v + EPS) * g + b
            return bn + alpha * x
        b, c, h, w = x.shape
        n = h * w
        hd = c // NH
        scale = hd ** (-0.5)
        t = x.reshape(b, c, n).transpose(0, 2, 1)
        qkv = (t @ Wqkv + bqkv).reshape(b, n, 3, NH, hd).transpose(2, 0, 3, 1, 4)
        q, k, v = (qkv[0], qkv[1], qkv[2])
        q = jax.nn.relu(q) * scale
        k = jax.nn.relu(k)
        ctx = jnp.einsum('bhnd,bhne->bhde', k, v)
        out = jnp.einsum('bhnd,bhde->bhne', q, ctx)
        out = out.transpose(0, 2, 1, 3).reshape(b, n, c)
        img = out.transpose(0, 2, 1).reshape(b, c, h, w)
        img = jax.lax.conv_general_dilated(img, dw_w, (1, 1), 'SAME', feature_group_count=c)
        img = img + dw_b[None, :, None, None]
        out = img.reshape(b, c, n).transpose(0, 2, 1)
        out = out @ Wproj + bproj
        t = _repbn(t + out, bn1_g, bn1_b, bn1_m, bn1_v, alpha1)
        ff = jax.nn.gelu(t @ Wfc1 + bfc1, approximate=False) @ Wfc2 + bfc2
        t = _repbn(t + ff, bn2_g, bn2_b, bn2_m, bn2_v, alpha2)
        return t.transpose(0, 2, 1).reshape(b, c, h, w)

    def _gn(v, G=32, eps=1e-05):
        B_, C_, H_, W_ = v.shape
        g = v.reshape(B_, G, C_ // G, H_, W_)
        m = jnp.mean(g, axis=(2, 3, 4), keepdims=True)
        s = jnp.var(g, axis=(2, 3, 4), keepdims=True)
        return ((g - m) / jnp.sqrt(s + eps)).reshape(v.shape)

    def _ln_c(v, eps=1e-06):
        m = jnp.mean(v, axis=1, keepdims=True)
        s = jnp.var(v, axis=1, keepdims=True)
        return (v - m) / jnp.sqrt(s + eps)

    def _ln_t(v, eps=1e-05):
        m = jnp.mean(v, axis=-1, keepdims=True)
        s = jnp.var(v, axis=-1, keepdims=True)
        return (v - m) / jnp.sqrt(s + eps)

    def _to_tokens(v):
        B_, C_, H_, W_ = v.shape
        return v.reshape(B_, C_, H_ * W_).transpose(0, 2, 1)

    def _from_tokens(t, like):
        B_, C_, H_, W_ = like.shape
        return t.transpose(0, 2, 1).reshape(B_, C_, H_, W_)
    x = x + _L0_conv_ref(_gn(x), L0_conv_ln_gamma, L0_conv_ln_beta, L0_conv_w_qkv, L0_conv_b_qkv, L0_conv_w_out, L0_conv_b_out)
    x = x + _L1_conv_ref(_gn(x), L1_conv_Wqkv, L1_conv_bqkv, L1_conv_dw_w, L1_conv_dw_b, L1_conv_Wproj, L1_conv_bproj, L1_conv_bn1_g, L1_conv_bn1_b, L1_conv_bn1_m, L1_conv_bn1_v, L1_conv_alpha1, L1_conv_Wfc1, L1_conv_bfc1, L1_conv_Wfc2, L1_conv_bfc2, L1_conv_bn2_g, L1_conv_bn2_b, L1_conv_bn2_m, L1_conv_bn2_v, L1_conv_alpha2)
    return x

_drawn_inputs = setup_inputs


def setup_inputs(seed=0):
    import zlib

    import numpy as np

    out = dict(_drawn_inputs(seed))
    spreads = {'L0_conv_ln_gamma': (1.0, 0.6),
     'L0_conv_ln_beta': (0.0, 0.1),
     'L0_conv_b_qkv': (0.0, 0.1),
     'L0_conv_b_out': (0.0, 0.1),
     'L1_conv_bn1_g': (1.0, 0.2),
     'L1_conv_bn1_b': (0.0, 0.1),
     'L1_conv_bn2_g': (1.0, 0.2),
     'L1_conv_bn2_b': (0.0, 0.398)}
    factors = {'L1_conv_dw_b': 8.0,
     'L1_conv_bproj': 3.263,
     'L1_conv_bn1_m': 6.448,
     'L1_conv_bfc1': 8.0,
     'L1_conv_bfc2': 7.736,
     'L1_conv_bn2_m': 8.0}
    for name, (base, spread) in spreads.items():
        noise = np.random.default_rng([zlib.crc32(name.encode()), seed]).standard_normal(out[name].shape)
        drawn = base * np.exp(spread * noise) if base else spread * noise
        out[name] = jnp.asarray(drawn.astype(out[name].dtype))
    for name, factor in factors.items():
        out[name] = (out[name] * factor).astype(out[name].dtype)
    return out
```

```python
from contextlib import ExitStack

import numpy as np
import concourse.bass as bass
from concourse import mybir

F32 = mybir.dt.float32
BF16 = mybir.dt.bfloat16
ALU = mybir.AluOpType
ACT = mybir.ActivationFunctionType
AX = mybir.AxisListType

P = 128
NIMG, C, H, W = 4, 128, 112, 112
HW = H * W
WIN, NH, HD = 8, 8, 16
STRIP_ROWS = WIN
STRIPS = H // STRIP_ROWS
STRIP = STRIP_ROWS * W
GROUP_PAIRS = (4, 3)
GROUP_FIRST = (0, 4)
GROUPS = 2 * STRIPS
QUADS = 4
VCOLS = 2 * (HD + 1)
BLOCK_ROWS = 4
BLOCK = BLOCK_ROWS * W
BLOCKS = H // BLOCK_ROWS
CM = 1024
NF = CM // P
QW = W + 2
KV_TILES = STRIP // P
KV_CHUNKS = ((0, 2), (2, 2), (4, 2), (6, 1))
TAPS = [(dy, dx) for dy in range(3) for dx in range(3)]
GN_EPS, LN_EPS, BN_EPS = 1e-5, 1e-5, 1e-5

VEC = ["gamma", "beta", "bq", "bk", "bout", "dwb", "bproj", "g1", "b1", "m1", "v1", "a1", "bfc2",
       "g2", "b2", "m2", "v2", "a2", "mask_lo", "mask_hi"]
NVEC = len(VEC)
WMATS = ["wq", "wk", "wv", "wout", "lwq", "lwk", "lwv", "wproj"]
CMATS = ["ident", "gmat", "cmask", "sel", "bias_v", "bias_lk", "bias_lv"]


def build(nc, x_d, vec_d, fc1b_d, dw_d, wm_d, cm_d, w1_d, w2_d, out_d):
    with ExitStack() as ctx:
        def sb(name, shape, dt=F32, stack=ctx):
            return stack.enter_context(nc.sbuf_tensor(name, shape, dt))

        def sem(name):
            return ctx.enter_context(nc.semaphore(name))

        ximg = sb("ximg", [P, HW])
        vec = sb("vec", [P, NVEC + 1])
        fc1b = sb("fc1b", [P, NF])
        dw = sb("dw", [P, 9])
        wm = sb("wm", [P, len(WMATS), P])
        cm = sb("cm", [P, len(CMATS), P])
        w1 = sb("w1", [P, CM])
        w2 = sb("w2", [P, NF, P])
        wp9 = sb("wp9", [P, 9, P])
        mtap = sb("mtap", [P, 9, P])
        ident16 = sb("ident16", [P, P], BF16)
        sel16 = sb("sel16", [P, P], BF16)
        neghalf = sb("neghalf", [P, 4])
        par = sb("par", [P, 16])
        gstats = sb("gstats", [P, GROUPS, 6])
        mv = sb("mv", [P, 2])
        gmv = sb("gmv", [P, 2])
        gdev = sb("gdev", [P, 2])
        gcoef = sb("gcoef", [P, 4])
        ctxt = sb("ctxt", [P, P])
        vx = sb("vx", [P, 2, 8, QUADS, VCOLS])
        mx = sb("mx", [P, 2, 4, QUADS, 32], BF16)

        def v(name, n=1):
            k = VEC.index(name)
            return vec[:, k:k + n]

        def wmat(name):
            return wm[:, WMATS.index(name), :]

        def cmat(name):
            return cm[:, CMATS.index(name), :]

        PAR = ["bq_s", "bk_lo", "bk_hi", "s1", "B1", "cb", "s2", "B2", "r1", "r2"]

        def par_(name):
            k = PAR.index(name)
            return par[:, k:k + 1]

        stack_b = ExitStack()
        xg = sb("xg", [P, 2, 512], F32, stack_b)
        lnst = sb("lnst", [P, 2, 4, 6], F32, stack_b)
        lnmv = sb("lnmv", [P, 2, 4, 2], F32, stack_b)
        lnve = sb("lnve", [P, 2, 4], F32, stack_b)
        lnrs = sb("lnrs", [P, 2, 4], F32, stack_b)
        xc = sb("xc", [P, 2, 512], F32, stack_b)
        xn = sb("xn", [P, 2, 512], F32, stack_b)
        qh = sb("qh", [P, 2, 512], F32, stack_b)
        kx = sb("kx", [P, 2, 8, 2, 64], F32, stack_b)
        q16 = sb("q16", [P, 2, 512], BF16, stack_b)
        k16 = sb("k16", [P, 2, 8, 2, 64], BF16, stack_b)
        mt16 = sb("mt16", [P, 2, 512], BF16, stack_b)
        prob = sb("prob", [P, QUADS, 512], F32, stack_b)
        rden = sb("rden", [P, 2, 4, 8], F32, stack_b)
        oh = sb("oh", [P, 2, 512], F32, stack_b)
        ot = sb("ot", [P, 2, 512], F32, stack_b)
        ob = sb("ob", [P, 2, 512], F32, stack_b)
        stack_b.close()
        stack_c = ctx.enter_context(ExitStack())
        qimg = sb("qimg", [P, (H + 2) * QW], F32, stack_c)
        tst = sb("tst", [P, 2, STRIP], F32, stack_c)
        kv = sb("kv", [P, 2, 2, 2, P], F32, stack_c)
        krel = sb("krel", [P, 2, 2, P], F32, stack_c)
        tb = sb("tb", [P, BLOCK], F32, stack_c)
        zb = sb("zb", [P, BLOCK], F32, stack_c)
        t1 = sb("t1", [P, 2, BLOCK], F32, stack_c)
        hb = sb("hb", [P, NF, BLOCK], F32, stack_c)
        z2 = sb("z2", [P, BLOCK], F32, stack_c)
        z3 = sb("z3", [P, BLOCK], F32, stack_c)
        yb = sb("yb", [P, 2, BLOCK], F32, stack_c)

        bank = [ctx.enter_context(nc.psum_tensor(f"bank{n}", [P, 512], F32)) for n in range(8)]

        consts_loaded = sem("consts_loaded")
        x_loaded = sem("x_loaded")
        ones_set = sem("ones_set")
        waits_passed = sem("waits_passed")
        consts_cast = sem("consts_cast")
        par_sq = sem("par_sq")
        par_chain = sem("par_chain")
        par_ready = sem("par_ready")
        cb_mm = sem("cb_mm")
        gst_ready = sem("gst_ready")
        gmv_ready = sem("gmv_ready")
        gmean_mm = sem("gmean_mm")
        gdev1 = sem("gdev1")
        gdev_ready = sem("gdev_ready")
        gvar_mm = sem("gvar_mm")
        gvar_ready = sem("gvar_ready")
        grs_ready = sem("grs_ready")
        gcoef_ready = sem("gcoef_ready")
        xg_ready = sem("xg_ready")
        xt_mm = sem("xt_mm")
        lnst_ready = sem("lnst_ready")
        lnmv_ready = sem("lnmv_ready")
        lnve_ready = sem("lnve_ready")
        lnrs_ready = sem("lnrs_ready")
        xc_ready = sem("xc_ready")
        xnt_mm = sem("xnt_mm")
        xn_ready = sem("xn_ready")
        q_mm = sem("q_mm")
        q_ready = sem("q_ready")
        k_mm = sem("k_mm")
        k_ready = sem("k_ready")
        v_mm = sem("v_mm")
        v_ready = sem("v_ready")
        qk16_ready = sem("qk16_ready")
        smax_mm = sem("smax_mm")
        max_ready = sem("max_ready")
        mt_mm = sem("mt_mm")
        mt_ready = sem("mt_ready")
        st_mm = sem("st_mm")
        prob_ready = sem("prob_ready")
        pv_mm = sem("pv_mm")
        rden_ready = sem("rden_ready")
        oh_ready = sem("oh_ready")
        ot_mm = sem("ot_mm")
        ot_ready = sem("ot_ready")
        out_mm = sem("out_mm")
        ob_ready = sem("ob_ready")
        x1_ready = sem("x1_ready")
        pad_ready = sem("pad_ready")
        tst_ready = sem("tst_ready")
        lq_mm = sem("lq_mm")
        lq_ready = sem("lq_ready")
        kv_mm = sem("kv_mm")
        kv_ready = sem("kv_ready")
        krel_ready = sem("krel_ready")
        ctx_mm = sem("ctx_mm")
        ctxt_ready = sem("ctxt_ready")
        mtap_mm = sem("mtap_mm")
        mtap_ready = sem("mtap_ready")
        tb_ready = sem("tb_ready")
        conv_mm = sem("conv_mm")
        zb_ready = sem("zb_ready")
        t1_ready = sem("t1_ready")
        h_mm = sem("h_mm")
        h_ready = sem("h_ready")
        ff_mm = sem("ff_mm")
        z2_ready = sem("z2_ready")
        t2_ready = sem("t2_ready")
        y_ready = sem("y_ready")
        y_stored = [sem(f"y_stored{n}") for n in range(2)]

        NCONST = 8

        def windows(s, gg):
            w0, n = 2 * GROUP_FIRST[gg], 2 * GROUP_PAIRS[gg]
            a = ximg[:, bass.ds(s * STRIP, STRIP)]
            return a.rearrange("p (r w c) -> p w r c", r=WIN, w=W // WIN)[:, w0:w0 + n]

        def by_window(t, gg):
            n = 2 * GROUP_PAIRS[gg]
            return t[:, 0:64 * n].rearrange("p (w r c) -> p w r c", r=WIN, c=WIN)

        def group_loop(eng, i, step, prologue=None, epilogue=None):
            if prologue:
                prologue(i * GROUPS)
            for gg in range(2):
                step(i * GROUPS + gg, 0, gg, gg == 0, False)
            with eng.Fori(1, STRIPS - 1) as s:
                for gg in range(2):
                    step(i * GROUPS + s * 2 + gg, s, gg, False, False)
            for gg in range(2):
                step(i * GROUPS + 2 * (STRIPS - 1) + gg, STRIPS - 1, gg, False, gg == 1)
            if epilogue:
                epilogue(i * GROUPS)

        def block_loop(eng, i, step):
            def strip(s):
                for bb in range(2):
                    step(i * BLOCKS + s * 2 + bb, s, s * 2 + bb, bb,
                         isinstance(s, int) and s == STRIPS - 1 and bb == 1)
            strip(0)
            with eng.Fori(1, STRIPS - 1) as s:
                strip(s)
            strip(STRIPS - 1)

        def hold(eng):
            eng.sem_inc(waits_passed, 1)

        block = ctx.enter_context(nc.Block())

        @block.sync
        def _(sp):
            for dst, src in ((vec, vec_d), (fc1b, fc1b_d), (dw, dw_d), (wm, wm_d), (cm, cm_d),
                             (w1, w1_d), (w2, w2_d)):
                sp.dma_start(dst[:], src).then_inc(consts_loaded, 16)
            for s in range(STRIPS):
                sp.dma_start(ximg[:, s * STRIP:(s + 1) * STRIP],
                             x_d[0, :, s * STRIP:(s + 1) * STRIP]).then_inc(x_loaded, 16)

            def store(i, b, bb, B):
                sp.wait_ge(y_ready, B + 1)
                sp.dma_start(out_d[bass.ds(i, 1), :, bass.ds(b * BLOCK, BLOCK)].rearrange("a p n -> p (a n)"),
                             yb[:, bb, :]).then_inc(y_stored[bb], 16)

            with sp.Fori(0, NIMG - 1) as i:
                def strip(s, last):
                    for bb in range(2):
                        store(i, s * 2 + bb, bb, i * BLOCKS + s * 2 + bb)
                    if last:
                        for bb in range(2):
                            sp.wait_ge(y_stored[bb], (i + 1) * (16 * STRIPS))
                    sp.dma_start(ximg[:, bass.ds(s * STRIP, STRIP)],
                                 x_d[bass.ds(i + 1, 1), :, bass.ds(s * STRIP, STRIP)]
                                 .rearrange("a p n -> p (a n)")).then_inc(x_loaded, 16)

                with sp.Fori(0, STRIPS - 1) as s:
                    strip(s, False)
                strip(STRIPS - 1, True)
            with sp.Fori(0, STRIPS) as s:
                for bb in range(2):
                    store(NIMG - 1, s * 2 + bb, bb, (NIMG - 1) * BLOCKS + s * 2 + bb)
            for bb in range(2):
                sp.wait_ge(y_stored[bb], 16 * NIMG * STRIPS)

        @block.gpsimd
        def _(pool):
            g = nc.gpsimd
            g.memset(neghalf[:], -0.5).then_inc(ones_set, 1)
            g.memset(vx[:], 0.0).then_inc(ones_set, 1)
            g.memset(mx[:], 0.0).then_inc(ones_set, 1)
            pool.wait_ge(ones_set, 3)
            pool.wait_ge(par_sq, 2)
            g.tensor_tensor(par_("r1"), par_("s1"), neghalf[:, 0:1], ALU.pow).then_inc(par_chain, 1)
            g.tensor_tensor(par_("r2"), par_("s2"), neghalf[:, 0:1], ALU.pow).then_inc(par_chain, 1)

            def gn_coef(n):
                pool.wait_ge(gvar_ready, n + 1)
                hold(pool)
                g.tensor_tensor(gcoef[:, 0:1], gdev[:, 1:2], neghalf[:, 0:1], ALU.pow).then_inc(grs_ready, 1)
                pool.wait_ge(grs_ready, n + 1)
                hold(pool)
                g.tensor_scalar(gcoef[:, 1:2], gmv[:, 0:1], -1.0, gcoef[:, 0:1], ALU.mult, ALU.mult)\
                    .then_inc(gcoef_ready, 1)

            def ln_rstd(G, gg):
                n = GROUP_PAIRS[gg]
                pool.wait_ge(lnmv_ready, G + 1)
                hold(pool)
                g.tensor_scalar_add(lnve[:, gg, 0:n], lnmv[:, gg, 0:n, 1], LN_EPS).then_inc(lnve_ready, 1)
                pool.wait_ge(lnve_ready, G + 1)
                g.tensor_tensor(lnrs[:, gg, 0:n], lnve[:, gg, 0:n], neghalf[:, 0:n], ALU.pow)\
                    .then_inc(lnrs_ready, 1)

            def cast_qk(G, gg):
                n = GROUP_PAIRS[gg]
                pool.wait_ge(q_ready, G + 1)
                hold(pool)
                g.tensor_copy(q16[:, gg, 0:P * n], qh[:, gg, 0:P * n])
                pool.wait_ge(k_ready, G + 1)
                hold(pool)
                g.tensor_copy(k16[:, gg, 0:2 * n], kx[:, gg, 0:2 * n]).then_inc(qk16_ready, 1)

            def prologue(G):
                ln_rstd(G, 0)
                cast_qk(G, 0)

            def residual(G, s, gg):
                pool.wait_ge(ob_ready, G + 1)
                hold(pool)
                xw = windows(s, gg)
                g.tensor_tensor(xw, xw, by_window(ob[:, gg, :], gg), ALU.add).then_inc(x1_ready, 1)

            def step(G, s, gg, first, last):
                if not last:
                    ln_rstd(G + 1, 1 - gg)
                if not first:
                    residual(G - 1, *((s - 1, 1) if gg == 0 else (s, 0)))
                if not last:
                    cast_qk(G + 1, 1 - gg)

            with pool.Fori(0, NIMG) as i:
                gn_coef(i * 2)
                group_loop(pool, i, step, prologue,
                           lambda G0: residual(G0 + GROUPS - 1, STRIPS - 1, 1))
                pool.wait_ge(x1_ready, (i + 1) * GROUPS)
                hold(pool)
                qv = qimg[:].rearrange("p (r c) -> p r c", c=QW)
                g.memset(qv[:, 0:1, :], 0.0)
                g.memset(qv[:, H + 1:H + 2, :], 0.0)
                g.memset(qv[:, 1:H + 1, 0:1], 0.0)
                g.memset(qv[:, 1:H + 1, QW - 1:QW], 0.0).then_inc(pad_ready, 1)
                gn_coef(i * 2 + 1)

        @block.scalar
        def _(act):
            a = nc.scalar
            act.wait_ge(par_ready, 1)

            def xn_evac(G, gg):
                n = P * GROUP_PAIRS[gg]
                act.wait_ge(xnt_mm, G + 1)
                a.activation(xn[:, gg, 0:n], bank[5][:, 0:n], ACT.Identity, bias=v("beta"),
                             scale=v("gamma")).then_inc(xn_ready, 1)

            def qk_evac(G, gg):
                n = P * GROUP_PAIRS[gg]
                act.wait_ge(q_mm, G + 1)
                a.activation(qh[:, gg, 0:n], bank[5][:, 0:n], ACT.Identity, bias=par_("bq_s"),
                             scale=float(HD) ** -0.5).then_inc(q_ready, 1)
                act.wait_ge(k_mm, G + 1)
                kp = bank[4][:, 0:n].rearrange("p (w k) -> p w k", k=64)
                a.activation(kx[:, gg, 0:n // 64, 0, :], kp, ACT.Identity, bias=par_("bk_lo"),
                             scale=v("mask_lo"))
                a.activation(kx[:, gg, 0:n // 64, 1, :], kp, ACT.Identity, bias=par_("bk_hi"),
                             scale=v("mask_hi")).then_inc(k_ready, 1)

            def exps(G, gg, first):
                n = P * GROUP_PAIRS[gg]
                if not first:
                    act.wait_ge(pv_mm, G)
                act.wait_ge(st_mm, G + 1)
                for j in range(QUADS):
                    e = a.activation(prob[:, j, 0:n], bank[j][:, 0:n], ACT.Exp)
                e.then_inc(prob_ready, 1)

            def ot_evac(G, gg):
                n = P * GROUP_PAIRS[gg]
                act.wait_ge(ot_mm, G + 1)
                a.activation(ot[:, gg, 0:n], bank[5][:, 0:n], ACT.Copy).then_inc(ot_ready, 1)

            def ob_evac(G, gg):
                n = P * GROUP_PAIRS[gg]
                act.wait_ge(out_mm, G + 1)
                a.activation(ob[:, gg, 0:n], bank[4][:, 0:n], ACT.Identity, bias=v("bout"))\
                    .then_inc(ob_ready, 1)

            def prologue(G):
                xn_evac(G, 0)
                qk_evac(G, 0)

            def step(G, s, gg, first, last):
                if not first:
                    ot_evac(G - 1, 1 - gg)
                if not last:
                    xn_evac(G + 1, 1 - gg)
                exps(G, gg, first)
                if not first:
                    ob_evac(G - 1, 1 - gg)
                if not last:
                    qk_evac(G + 1, 1 - gg)

            def epilogue(G0):
                ot_evac(G0 + GROUPS - 1, 1)
                ob_evac(G0 + GROUPS - 1, 1)

            with act.Fori(0, NIMG) as i:
                group_loop(act, i, step, prologue, epilogue)

                act.wait_ge(pad_ready, i + 1)

                def krel_evac(K, cc, n):
                    act.wait_ge(kv_ready, K + 1)
                    a.activation(krel[:, cc % 2, 0:n, :], kv[:, cc % 2, 0:n, 0, :], ACT.Relu)\
                        .then_inc(krel_ready, 1)

                def strip_c(s, first):
                    for bb in range(2):
                        B = i * BLOCKS + s * 2 + bb
                        act.wait_ge(lq_mm, B + 1)
                        rows = qimg[:, bass.ds((s * 2 + bb) * (BLOCK_ROWS * QW) + QW, BLOCK_ROWS * QW)]
                        a.activation(rows.rearrange("p (r c) -> p r c", c=QW)[:, :, 1:W + 1],
                                     bank[4 + bb][:, 0:BLOCK].rearrange("p (r c) -> p r c", c=W),
                                     ACT.Relu, bias=vec[:, NVEC:NVEC + 1]).then_inc(lq_ready, 1)
                    for cc, (_, n) in enumerate(KV_CHUNKS):
                        K = (i * STRIPS + s) * len(KV_CHUNKS) + cc
                        if not (first and cc < 2):
                            act.wait_ge(ctx_mm, K - 1)
                        krel_evac(K, cc, n)

                strip_c(0, True)
                with act.Fori(1, STRIPS) as s:
                    strip_c(s, False)

                act.wait_ge(mtap_mm, i + 1)
                for t in range(3):
                    m = a.activation(mtap[:, 3 * t:3 * t + 3, :],
                                     bank[t][:, 0:3 * P].rearrange("p (t o) -> p t o", o=P), ACT.Copy)
                m.then_inc(mtap_ready, 1)

                def step_d(B, s, b, bb, last):
                    for j in range(NF):
                        act.wait_ge(h_mm, B * NF + j + 1)
                        a.activation(hb[:, j, :], bank[j % 4][:, 0:BLOCK], ACT.Gelu,
                                     bias=fc1b[:, j:j + 1]).then_inc(h_ready, 1)

                block_loop(act, i, step_d)

        @block.vector
        def _(dve):
            d = nc.vector
            dve.wait_ge(consts_loaded, 16 * 7)
            d.tensor_copy(ident16[:], cmat("ident"))
            d.tensor_copy(sel16[:], cmat("sel")).then_inc(consts_cast, 1)
            for t in range(9):
                d.tensor_scalar(wp9[:, t, :], wmat("wproj"), dw[:, t:t + 1], None, ALU.mult)
            d.tensor_scalar(par_("bq_s"), v("bq"), float(HD) ** -0.5, None, ALU.mult)
            d.tensor_tensor(par_("bk_lo"), v("bk"), v("mask_lo"), ALU.mult)
            d.tensor_tensor(par_("bk_hi"), v("bk"), v("mask_hi"), ALU.mult)
            d.tensor_scalar(par_("s1"), v("v1"), BN_EPS, None, ALU.add).then_inc(par_sq, 1)
            d.tensor_scalar(par_("s2"), v("v2"), BN_EPS, None, ALU.add).then_inc(par_sq, 1)
            dve.wait_ge(ones_set, 3)
            for s in range(2):
                c = (HD + 1) * s + HD
                for b in range(2):
                    d.memset(vx[64 * s:64 * s + 64, b, :, :, c:c + 1], 1.0)
            dve.wait_ge(par_chain, 2)
            d.tensor_tensor(par_("r1"), par_("r1"), v("g1"), ALU.mult)
            d.tensor_tensor(par_("r2"), par_("r2"), v("g2"), ALU.mult).then_inc(par_chain, 1)
            dve.wait_ge(par_chain, 3)
            d.tensor_tensor(par_("B1"), v("m1"), par_("r1"), ALU.mult)
            d.tensor_tensor(par_("B2"), v("m2"), par_("r2"), ALU.mult)
            d.tensor_tensor(par_("s1"), par_("r1"), v("a1"), ALU.add)
            d.tensor_tensor(par_("s2"), par_("r2"), v("a2"), ALU.add).then_inc(par_chain, 1)
            dve.wait_ge(par_chain, 4)
            d.tensor_tensor(par_("B1"), v("b1"), par_("B1"), ALU.subtract)
            d.tensor_tensor(par_("B2"), v("b2"), par_("B2"), ALU.subtract)
            dve.wait_ge(cb_mm, 1)
            d.tensor_tensor(par_("cb"), bank[7][:, 0:1], v("bproj"), ALU.add).then_inc(par_ready, 1)
            dve.wait_ge(par_ready, 1)

            def group_norm(n):
                dve.wait_ge(gst_ready, n + 1)
                hold(dve)
                d.bn_aggr(mv[:], gstats[:]).then_inc(gmv_ready, 1)
                dve.wait_ge(gmean_mm, n + 1)
                d.tensor_copy(gmv[:], bank[7][:, 0:2]).then_inc(gdev1, 1)
                dve.wait_ge(gdev1, n * 2 + 1)
                d.tensor_tensor(gdev[:, 0:1], mv[:, 0:1], gmv[:, 0:1], ALU.subtract).then_inc(gdev1, 1)
                dve.wait_ge(gdev1, n * 2 + 2)
                d.tensor_tensor(gdev[:, 0:1], gdev[:, 0:1], gdev[:, 0:1], ALU.mult).then_inc(gdev_ready, 1)
                dve.wait_ge(gvar_mm, n + 1)
                d.scalar_tensor_tensor(gdev[:, 1:2], bank[7][:, 2:3], GN_EPS, gmv[:, 1:2], ALU.add,
                                       ALU.add).then_inc(gvar_ready, 1)

            def gn_apply(G, s, gg):
                d.tensor_scalar(by_window(xg[:, gg, :], gg), windows(s, gg), gcoef[:, 0:1],
                                gcoef[:, 1:2], ALU.mult, ALU.add).then_inc(xg_ready, 1)

            def ln_stats(G, gg):
                n = GROUP_PAIRS[gg]
                dve.wait_ge(xt_mm, G + 1)
                for t in range(n):
                    m = d.bn_stats(lnst[:, gg, t, :], bank[4][:, P * t:P * t + P])
                m.then_inc(lnst_ready, 1)
                dve.wait_ge(lnst_ready, G + 1)
                hold(dve)
                for t in range(n):
                    m = d.bn_aggr(lnmv[:, gg, t, :], lnst[:, gg, t, :])
                m.then_inc(lnmv_ready, 1)

            def ln_norm(G, gg):
                n = GROUP_PAIRS[gg]
                dve.wait_ge(lnrs_ready, G + 1)
                for t in range(n):
                    m = d.tensor_scalar(xc[:, gg, P * t:P * t + P], bank[4][:, P * t:P * t + P],
                                        lnmv[:, gg, t, 0:1], lnrs[:, gg, t:t + 1], ALU.subtract, ALU.mult)
                m.then_inc(xc_ready, 1)

            def v_evac(G, gg):
                n = GROUP_PAIRS[gg]
                dve.wait_ge(v_mm, G + 1)
                for w2 in range(2):
                    rows = slice(64 * w2, 64 * w2 + 64)
                    for s in range(2):
                        src = bank[5][rows, 0:P * n].rearrange("p (t j s d) -> p t j s d", j=QUADS, s=2,
                                                               d=HD)[:, :, :, s, :]
                        bias = cmat("bias_v")[rows].rearrange("p (t j s d) -> p t j s d", t=1, j=QUADS, s=2,
                                                              d=HD)[:, :, :, s, :]
                        dst = vx[64 * s:64 * s + 64, gg, w2:2 * n:2, :, (HD + 1) * s:(HD + 1) * s + HD]
                        m = d.tensor_tensor(dst, src, bias.to_broadcast([64, n, QUADS, HD]), ALU.add)
                m.then_inc(v_ready, 1)

            def maxima(G, gg):
                n = GROUP_PAIRS[gg]
                dve.wait_ge(smax_mm, G + 1)
                for j in range(QUADS):
                    m = d.tensor_reduce(mx[:, gg, 0:n, j, 0:2],
                                        bank[j][:, 0:P * n].rearrange("p (t s k) -> p t s k", s=2, k=64),
                                        AX.X, ALU.max)
                m.then_inc(max_ready, 1)

            def mt_evac(G, gg):
                n = P * GROUP_PAIRS[gg]
                dve.wait_ge(mt_mm, G + 1)
                d.tensor_copy(mt16[:, gg, 0:n], bank[4][:, 0:n // 2].bitcast(BF16)).then_inc(mt_ready, 1)

            def normalise(G, gg):
                n = GROUP_PAIRS[gg]
                dve.wait_ge(pv_mm, G + 1)

                def part(h):
                    k = min(2, n - 2 * h)
                    return k, bank[6 + h][:, 0:k * QUADS * VCOLS].rearrange("p (t e c) -> p t e c", e=8, c=HD + 1)
                for h in range(2):
                    k, src = part(h)
                    m = d.reciprocal(rden[:, gg, 2 * h:2 * h + k, :], src[:, :, :, HD])
                m.then_inc(rden_ready, 1)
                dve.wait_ge(rden_ready, G + 1)
                for h in range(2):
                    k, src = part(h)
                    r = rden[:, gg, 2 * h:2 * h + k, :].unsqueeze(3).to_broadcast([P, k, 8, HD])
                    dst = oh[:, gg, 2 * P * h:2 * P * h + P * k].rearrange("p (t e c) -> p t e c", e=8, c=HD)
                    m = d.tensor_tensor(dst, src[:, :, :, 0:HD], r, ALU.mult)
                m.then_inc(oh_ready, 1)

            def prologue(G):
                gn_apply(G, 0, 0)
                gn_apply(G + 1, 0, 1)
                ln_stats(G, 0)
                ln_norm(G, 0)
                v_evac(G, 0)

            def strip_stats(s, G):
                dve.wait_ge(x1_ready, G)
                for h in range(2):
                    src = ximg[:, bass.ds(s * STRIP + h * BLOCK, BLOCK)]
                    m = d.bn_stats(gstats[:, bass.ds(s * 2 + h, 1), :].rearrange("p a c -> p (a c)"), src)
                return m

            def step(G, s, gg, first, last):
                if not last:
                    ln_stats(G + 1, 1 - gg)
                maxima(G, gg)
                if not last:
                    ln_norm(G + 1, 1 - gg)
                if not first:
                    normalise(G - 1, 1 - gg)
                mt_evac(G, gg)
                if not last:
                    v_evac(G + 1, 1 - gg)
                if gg == 1 and not (isinstance(s, int) and s == 0):
                    strip_stats(s - 1, G - 1)
                if not (isinstance(s, int) and s == STRIPS - 1):
                    gn_apply(G + 2, s + 1, gg)

            def epilogue(G0):
                normalise(G0 + GROUPS - 1, 1)
                strip_stats(STRIPS - 1, G0 + GROUPS).then_inc(gst_ready, 1)

            with dve.Fori(0, NIMG) as i:
                dve.wait_ge(x_loaded, (i + 1) * (16 * STRIPS))
                hold(dve)
                with dve.Fori(0, GROUPS) as h:
                    d.bn_stats(gstats[:, bass.ds(h, 1), :].rearrange("p a c -> p (a c)"),
                               ximg[:, bass.ds(h * BLOCK, BLOCK)])
                d.engine_nop().then_inc(gst_ready, 1)
                group_norm(i * 2)
                dve.wait_ge(gcoef_ready, i * 2 + 1)
                hold(dve)
                group_loop(dve, i, step, prologue, epilogue)
                group_norm(i * 2 + 1)

                dve.wait_ge(gcoef_ready, i * 2 + 2)
                hold(dve)

                def norm_strip(s, sp):
                    d.tensor_scalar(tst[:, sp, :], ximg[:, bass.ds(s * STRIP, STRIP)], gcoef[:, 0:1],
                                    gcoef[:, 1:2], ALU.mult, ALU.add).then_inc(tst_ready, 1)

                def strip_c(s, first):
                    for cc, (_, n) in enumerate(KV_CHUNKS):
                        K = (i * STRIPS + s) * len(KV_CHUNKS) + cc
                        dve.wait_ge(kv_mm, K + 1)
                        if not (first and cc < 2):
                            dve.wait_ge(ctx_mm, K - 1)
                        src = bank[2 + cc % 2][:, 0:2 * P * n].rearrange("p (t c) -> p t c", c=2 * P)
                        bias = cm[:, CMATS.index("bias_lk"):CMATS.index("bias_lk") + 2, :]\
                            .rearrange("p (a b) c -> p a (b c)", a=1).to_broadcast([P, n, 2 * P])
                        d.tensor_tensor(kv[:, cc % 2, 0:n].rearrange("p t b c -> p t (b c)"), src, bias,
                                        ALU.add).then_inc(kv_ready, 1)

                norm_strip(0, 0)
                norm_strip(1, 1)
                strip_c(0, True)
                norm_strip(2, 0)
                strip_c(1, False)
                with dve.Fori(1, STRIPS // 2 - 1) as h:
                    for sp in range(2):
                        norm_strip(h * 2 + sp + 1, 1 - sp)
                        strip_c(h * 2 + sp, False)
                norm_strip(STRIPS - 1, 1)
                strip_c(STRIPS - 2, False)
                strip_c(STRIPS - 1, False)
                dve.wait_ge(ctx_mm, (i + 1) * (STRIPS * len(KV_CHUNKS)))
                d.tensor_tensor(ctxt[:], bank[6][:, 0:P], cmat("cmask"), ALU.mult).then_inc(ctxt_ready, 1)

                def mix(B, b, bb):
                    d.tensor_scalar(tb[:], ximg[:, bass.ds(b * BLOCK, BLOCK)], gcoef[:, 0:1],
                                    gcoef[:, 1:2], ALU.mult, ALU.add).then_inc(tb_ready, 1)
                    dve.wait_ge(tb_ready, B + 1)
                    dve.wait_ge(conv_mm, B + 1)
                    d.scalar_tensor_tensor(zb[:], bank[4 + bb][:, 0:BLOCK], par_("cb"), tb[:], ALU.add,
                                           ALU.add).then_inc(zb_ready, 1)
                    dve.wait_ge(zb_ready, B + 1)
                    d.tensor_scalar(t1[:, bb, :], zb[:], par_("s1"), par_("B1"), ALU.mult, ALU.add)\
                        .then_inc(t1_ready, 1)

                def step_d(B, s, b, bb, last):
                    if not last:
                        mix(B + 1, b + 1, 1 - bb)
                    dve.wait_ge(ff_mm, B + 1)
                    d.scalar_tensor_tensor(z2[:], bank[6 + bb][:, 0:BLOCK], v("bfc2"), t1[:, bb, :],
                                           ALU.add, ALU.add).then_inc(z2_ready, 1)
                    dve.wait_ge(z2_ready, B + 1)
                    d.tensor_scalar(z3[:], z2[:], par_("s2"), par_("B2"), ALU.mult, ALU.add)\
                        .then_inc(t2_ready, 1)
                    if not (isinstance(b, int) and b < 2):
                        dve.wait_ge(y_stored[bb], (i * STRIPS + s) * 16)
                    dve.wait_ge(t2_ready, B + 1)
                    d.tensor_tensor(yb[:, bb, :], z3[:], ximg[:, bass.ds(b * BLOCK, BLOCK)],
                                    ALU.add).then_inc(y_ready, 1)

                mix(i * BLOCKS, 0, 0)
                block_loop(dve, i, step_d)

        @block.tensor
        def _(pe):
            mm = nc.tensor.matmul
            tr = nc.tensor.transpose
            pe.wait_ge(consts_loaded, 16 * 7)
            pe.wait_ge(consts_cast, 1)
            mm(bank[7][:, 0:1], wmat("wproj"), v("dwb"), start=True, stop=True).then_inc(cb_mm, 1)

            def group_norm(n):
                pe.wait_ge(gmv_ready, n + 1)
                mm(bank[7][:, 0:2], cmat("gmat"), mv[:], start=True, stop=True).then_inc(gmean_mm, 1)
                pe.wait_ge(gdev_ready, n + 1)
                mm(bank[7][:, 2:3], cmat("gmat"), gdev[:, 0:1], start=True, stop=True).then_inc(gvar_mm, 1)

            def ln_transpose(G, gg):
                pe.wait_ge(xg_ready, G + 1)
                for t in range(GROUP_PAIRS[gg]):
                    m = tr(bank[4][:, P * t:P * t + P], xg[:, gg, P * t:P * t + P], cmat("ident"))
                m.then_inc(xt_mm, 1)

            def ln_back(G, gg):
                pe.wait_ge(xc_ready, G + 1)
                for t in range(GROUP_PAIRS[gg]):
                    m = tr(bank[5][:, P * t:P * t + P], xc[:, gg, P * t:P * t + P], cmat("ident"))
                m.then_inc(xnt_mm, 1)

            def project(G, gg):
                n = P * GROUP_PAIRS[gg]
                pe.wait_ge(xn_ready, G + 1)
                mm(bank[5][:, 0:n], wmat("wq"), xn[:, gg, 0:n], start=True, stop=True).then_inc(q_mm, 1)
                mm(bank[4][:, 0:n], wmat("wk"), xn[:, gg, 0:n], start=True, stop=True).then_inc(k_mm, 1)
                pe.wait_ge(q_ready, G + 1)
                for t in range(GROUP_PAIRS[gg]):
                    m = mm(bank[5][:, P * t:P * t + P], xn[:, gg, P * t:P * t + P], wmat("wv"),
                           start=True, stop=True)
                m.then_inc(v_mm, 1)

            def score_rows(G, gg):
                pe.wait_ge(qk16_ready, G + 1)
                for w in range(2 * GROUP_PAIRS[gg]):
                    t, w2 = w // 2, w % 2
                    for j in range(QUADS):
                        r = slice(32 * j, 32 * j + 32)
                        m = mm(bank[j][64 * w2:64 * w2 + 64, P * t:P * t + P],
                               q16[r, gg, 64 * w:64 * w + 64],
                               k16[r, gg, w, :, :].rearrange("p s k -> p (s k)"), start=True, stop=True)
                m.then_inc(smax_mm, 1)

            def score_cols(G, gg):
                n = GROUP_PAIRS[gg]
                pe.wait_ge(max_ready, G + 1)
                b4 = bank[4][:, 0:256].bitcast(BF16)
                for t in range(n):
                    m = tr(b4[:, P * t:P * t + P], mx[:, gg, t].rearrange("p j c -> p (j c)"), ident16[:])
                m.then_inc(mt_mm, 1)

            def score_cols2(G, gg):
                n = GROUP_PAIRS[gg]
                pe.wait_ge(mt_ready, G + 1)
                for j in range(QUADS):
                    r = slice(32 * j, 32 * j + 32)
                    mm(bank[j][:, 0:P * n], sel16[r, :], mt16[r, gg, 0:P * n], start=True, stop=True,
                       skip_group_check=True)
                for w in range(2 * n):
                    for j in range(QUADS):
                        r = slice(32 * j, 32 * j + 32)
                        m = mm(bank[j][:, 64 * w:64 * w + 64],
                               kx[r, gg, w, :, :].rearrange("p s k -> p (s k)"),
                               qh[r, gg, 64 * w:64 * w + 64], start=False, stop=True,
                               skip_group_check=True)
                m.then_inc(st_mm, 1)

            def attend(G, gg):
                pe.wait_ge(prob_ready, G + 1)
                for w in range(2 * GROUP_PAIRS[gg]):
                    t, w2 = w // 2, w % 2
                    for j in range(QUADS):
                        c = (t % 2) * QUADS * VCOLS + j * VCOLS
                        m = mm(bank[6 + t // 2][64 * w2:64 * w2 + 64, c:c + VCOLS],
                               prob[:, j, 64 * w:64 * w + 64], vx[:, gg, w, j, :], start=True, stop=True)
                m.then_inc(pv_mm, 1)

            def out_transpose(G, gg):
                pe.wait_ge(oh_ready, G + 1)
                for t in range(GROUP_PAIRS[gg]):
                    m = tr(bank[5][:, P * t:P * t + P], oh[:, gg, P * t:P * t + P], cmat("ident"))
                m.then_inc(ot_mm, 1)

            def out_project(G, gg):
                n = P * GROUP_PAIRS[gg]
                pe.wait_ge(ot_ready, G + 1)
                mm(bank[4][:, 0:n], wmat("wout"), ot[:, gg, 0:n], start=True, stop=True).then_inc(out_mm, 1)

            def prologue(G):
                ln_transpose(G, 0)
                ln_back(G, 0)
                project(G, 0)

            def step(G, s, gg, first, last):
                ng = 1 - gg
                if not first:
                    pe.wait_ge(prob_ready, G)
                score_rows(G, gg)
                if not last:
                    ln_transpose(G + 1, ng)
                if not first:
                    pe.wait_ge(v_ready, G)
                    attend(G - 1, ng)
                    pe.wait_ge(v_ready, G + 1)
                    out_transpose(G - 1, ng)
                if not last:
                    pe.wait_ge(xc_ready, G + 2)
                score_cols(G, gg)
                if not last:
                    if not first:
                        pe.wait_ge(ot_ready, G)
                    else:
                        pe.wait_ge(v_ready, G + 1)
                    ln_back(G + 1, ng)
                score_cols2(G, gg)
                if not first:
                    out_project(G - 1, ng)
                if not last:
                    if not first:
                        pe.wait_ge(ob_ready, G)
                    project(G + 1, ng)

            def epilogue(G0):
                G = G0 + GROUPS - 1
                attend(G, 1)
                out_transpose(G, 1)
                out_project(G, 1)

            with pe.Fori(0, NIMG) as i:
                group_norm(i * 2)
                group_loop(pe, i, step, prologue, epilogue)
                group_norm(i * 2 + 1)
                pe.wait_ge(ob_ready, (i + 1) * GROUPS)

                def lq(s, sp, bb):
                    B = i * BLOCKS + s * 2 + bb
                    mm(bank[4 + bb][:, 0:BLOCK], wmat("lwq"), tst[:, sp, bb * BLOCK:(bb + 1) * BLOCK],
                       start=True, stop=True).then_inc(lq_mm, 1)

                def lkv(sp, cc):
                    t0, n = KV_CHUNKS[cc]
                    for t in range(n):
                        m = mm(bank[2 + cc % 2][:, 2 * P * t:2 * P * t + 2 * P],
                               tst[:, sp, P * (t0 + t):P * (t0 + t) + P],
                               wm[:, WMATS.index("lwk"):WMATS.index("lwk") + 2, :].rearrange("p a b -> p (a b)"),
                               start=True, stop=True)
                    m.then_inc(kv_mm, 1)

                def context(K, cc, first=False, last=False):
                    n = KV_CHUNKS[cc][1]
                    pe.wait_ge(krel_ready, K + 1)
                    for t in range(n):
                        m = mm(bank[6][:, 0:P], kv[:, cc % 2, t, 1, :], krel[:, cc % 2, t, :],
                               start=(first and t == 0), stop=(last and t == n - 1), skip_group_check=True)
                    m.then_inc(ctx_mm, 1)

                def strip_c(s, sp, first):
                    K0 = (i * STRIPS + s) * len(KV_CHUNKS)
                    pe.wait_ge(tst_ready, i * STRIPS + s + 1)
                    for bb in range(2):
                        if not first:
                            pe.wait_ge(lq_ready, i * BLOCKS + s * 2 + bb - 1)
                        lq(s, sp, bb)
                    for cc in range(len(KV_CHUNKS)):
                        if cc >= 2:
                            pe.wait_ge(kv_ready, K0 + cc - 1)
                        elif not first:
                            pe.wait_ge(kv_ready, K0 + cc - 1)
                        lkv(sp, cc)
                        if cc > 0:
                            context(K0 + cc - 1, cc - 1, first=(first and cc == 1))
                        elif not first:
                            context(K0 - 1, len(KV_CHUNKS) - 1)

                strip_c(0, 0, True)
                strip_c(1, 1, False)
                with pe.Fori(1, STRIPS // 2) as h:
                    for sp in range(2):
                        strip_c(h * 2 + sp, sp, False)
                context((i + 1) * (STRIPS * len(KV_CHUNKS)) - 1, len(KV_CHUNKS) - 1, last=True)

                pe.wait_ge(ctxt_ready, i + 1)
                for t in range(3):
                    m = mm(bank[t][:, 0:3 * P], ctxt[:], wp9[:, 3 * t:3 * t + 3, :].rearrange("p a b -> p (a b)"),
                           start=True, stop=True)
                m.then_inc(mtap_mm, 1)
                pe.wait_ge(lq_ready, (i + 1) * BLOCKS)
                pe.wait_ge(mtap_ready, i + 1)

                def conv(B, b, bb):
                    for t, (dy, dx) in enumerate(TAPS):
                        src = qimg[:, bass.ds(b * (BLOCK_ROWS * QW) + dy * QW, BLOCK_ROWS * QW)]\
                            .rearrange("p (r c) -> p r c", c=QW)[:, :, dx:dx + W]
                        m = mm(bank[4 + bb][:, 0:BLOCK], mtap[:, t, :], src, start=(t == 0), stop=(t == 8))
                    m.then_inc(conv_mm, 1)

                def fc1(B, bb, j):
                    pe.wait_ge(h_ready, B * NF + j - 3) if j >= 4 else None
                    mm(bank[j % 4][:, 0:BLOCK], w1[:, P * j:P * j + P], t1[:, bb, :], start=True,
                       stop=True).then_inc(h_mm, 1)

                def fc2(B, bb, j):
                    pe.wait_ge(h_ready, B * NF + j + 1)
                    m = mm(bank[6 + bb][:, 0:BLOCK], w2[:, j, :], hb[:, j, :], start=(j == 0),
                           stop=(j == NF - 1))
                    if j == NF - 1:
                        m.then_inc(ff_mm, 1)

                LAG = 3

                def step_d(B, s, b, bb, last):
                    pe.wait_ge(t1_ready, B + 1)
                    for j in range(NF):
                        fc1(B, bb, j)
                        if j >= LAG:
                            fc2(B, bb, j - LAG)
                    if not last:
                        conv(B + 1, b + 1, 1 - bb)
                    for j in range(NF - LAG, NF):
                        fc2(B, bb, j)

                conv(i * BLOCKS, 0, 0)
                block_loop(pe, i, step_d)


NVEC_LBQ = NVEC


_HEAD_ORDER = np.concatenate([np.arange(HD) + HD * (j + 4 * s) for j in range(QUADS) for s in range(2)])


def _constants():
    eye = np.eye(P, dtype=np.float32)
    grp = np.arange(P) // (C // 32)
    gmat = (grp[:, None] == grp[None, :]).astype(np.float32) * np.float32(0.25)
    head = np.arange(P) // HD
    cmask = (head[:, None] == head[None, :]).astype(np.float32) * np.float32(HD ** -0.5)
    sel = np.zeros((P, P), np.float32)
    for j in range(QUADS):
        for s in range(2):
            sel[32 * j + s, 64 * s:64 * s + 64] = -1.0
    mask_lo = ((np.arange(P) // HD) % 2 == 0).astype(np.float32)
    return eye, gmat, cmask, sel, mask_lo, np.float32(1) - mask_lo


def kernel(**inputs):
    import concourse.bacc as _bacc
    from concourse.bass_utils import run_bass_kernel_spmd as _run

    a = {k: np.asarray(t) for k, t in inputs.items()}
    eye, gmat, cmask, sel, mask_lo, mask_hi = _constants()
    o = _HEAD_ORDER
    wqkv, bqkv = a["L0_conv_w_qkv"], a["L0_conv_b_qkv"]
    lw, lb = a["L1_conv_Wqkv"], a["L1_conv_bqkv"]
    col = {
        "gamma": a["L0_conv_ln_gamma"], "beta": a["L0_conv_ln_beta"], "bq": bqkv[0:C][o],
        "bk": bqkv[C:2 * C][o], "bout": a["L0_conv_b_out"], "dwb": a["L1_conv_dw_b"],
        "bproj": a["L1_conv_bproj"], "g1": a["L1_conv_bn1_g"], "b1": a["L1_conv_bn1_b"],
        "m1": a["L1_conv_bn1_m"], "v1": a["L1_conv_bn1_v"], "a1": np.broadcast_to(a["L1_conv_alpha1"], (C,)),
        "bfc2": a["L1_conv_bfc2"], "g2": a["L1_conv_bn2_g"], "b2": a["L1_conv_bn2_b"],
        "m2": a["L1_conv_bn2_m"], "v2": a["L1_conv_bn2_v"],
        "a2": np.broadcast_to(a["L1_conv_alpha2"], (C,)), "mask_lo": mask_lo, "mask_hi": mask_hi,
    }
    vec = np.stack([col[n] for n in VEC] + [lb[0:C]], axis=1)
    wmats = {
        "wq": wqkv[0:C][o].T, "wk": wqkv[C:2 * C][o].T, "wv": wqkv[2 * C:][o].T,
        "wout": a["L0_conv_w_out"][:, o].T, "lwq": lw[:, 0:C], "lwk": lw[:, C:2 * C],
        "lwv": lw[:, 2 * C:], "wproj": a["L1_conv_Wproj"],
    }
    cmats = {
        "ident": eye, "gmat": gmat, "cmask": cmask, "sel": sel,
        "bias_v": np.broadcast_to(bqkv[2 * C:][o], (P, C)),
        "bias_lk": np.broadcast_to(lb[C:2 * C], (P, C)), "bias_lv": np.broadcast_to(lb[2 * C:], (P, C)),
    }
    arrays = {
        "x_in": a["x"].reshape(NIMG, C, HW),
        "vec_in": vec,
        "fc1b_in": a["L1_conv_bfc1"].reshape(NF, P).T,
        "dw_in": a["L1_conv_dw_w"].reshape(C, 9),
        "wm_in": np.stack([wmats[n] for n in WMATS], axis=1),
        "cm_in": np.stack([cmats[n] for n in CMATS], axis=1),
        "w1_in": a["L1_conv_Wfc1"],
        "w2_in": a["L1_conv_Wfc2"].reshape(NF, P, C).transpose(1, 0, 2),
    }
    arrays = {k: np.ascontiguousarray(t) for k, t in arrays.items()}
    nc = _bacc.Bacc("TRN2", target_bir_lowering=False, num_devices=1)
    args = [nc.dram_tensor(k, t.shape, mybir.dt.from_np(t.dtype), kind="ExternalInput").ap()
            for k, t in arrays.items()]
    args.append(nc.dram_tensor("y_out", (NIMG, C, HW), F32, kind="ExternalOutput").ap())
    build(nc, *args)
    r = _run(nc, [arrays], core_ids=[0])
    return r.results[0]["y_out"].reshape(NIMG, C, H, W)
```

```python
from contextlib import ExitStack

import numpy as np
import concourse.bass as bass
from concourse import mybir

F32 = mybir.dt.float32
BF16 = mybir.dt.bfloat16
ALU = mybir.AluOpType
ACT = mybir.ActivationFunctionType
AX = mybir.AxisListType

P = 128
NIMG, C, H, W = 4, 128, 112, 112
HW = H * W
WIN, NH, HD = 8, 8, 16
STRIP_ROWS = WIN
STRIPS = H // STRIP_ROWS
STRIP = STRIP_ROWS * W
GROUP_PAIRS = (4, 3)
GROUP_FIRST = (0, 4)
GROUPS = 2 * STRIPS
QUADS = 4
VCOLS = 2 * (HD + 1)
BLOCK_ROWS = 4
BLOCK = BLOCK_ROWS * W
BLOCKS = H // BLOCK_ROWS
CM = 1024
NF = CM // P
QW = W + 2
KV_TILES = STRIP // P
KV_CHUNKS = ((0, 2), (2, 2), (4, 2), (6, 1))
TAPS = [(dy, dx) for dy in range(3) for dx in range(3)]
GN_EPS, LN_EPS, BN_EPS = 1e-5, 1e-5, 1e-5

VEC = ["gamma", "beta", "bq", "bk", "bout", "dwb", "bproj", "g1", "b1", "m1", "v1", "a1", "bfc2",
       "g2", "b2", "m2", "v2", "a2", "mask_lo", "mask_hi", "bv", "blq"]
NVEC = len(VEC)
WMATS = ["wq", "wk", "wv", "wout", "lwq", "lwk", "lwv", "wproj"]
CMATS = ["ident", "gmat", "cmask", "bias_lk", "bias_lv"]


def build(nc, x_d, vec_d, fc1b_d, dw_d, wm_d, cm_d, w1_d, w2_d, sel_d, out_d):
    with ExitStack() as ctx:
        def sb(name, shape, dt=F32, stack=ctx):
            return stack.enter_context(nc.sbuf_tensor(name, shape, dt))

        def sem(name):
            return ctx.enter_context(nc.semaphore(name))

        ximg = sb("ximg", [P, HW])
        vec = sb("vec", [P, NVEC])
        fc1b = sb("fc1b", [P, NF])
        dw = sb("dw", [P, 9])
        wm = sb("wm", [P, len(WMATS), P])
        cm = sb("cm", [P, len(CMATS), P])
        w1 = sb("w1", [P, CM])
        w2 = sb("w2", [P, NF, P])
        wp9 = sb("wp9", [P, 9, P])
        mtap = sb("mtap", [P, 9, P])
        ident16 = sb("ident16", [P, P], BF16)
        sel16 = sb("sel16", [32, 16, P], BF16)
        neghalf = sb("neghalf", [P, 4])
        par = sb("par", [P, 16])
        gstats = sb("gstats", [P, GROUPS, 6])
        mv = sb("mv", [P, 2])
        gmv = sb("gmv", [P, 2])
        gdev = sb("gdev", [P, 2])
        gcoef = sb("gcoef", [P, 4])
        ctxt = sb("ctxt", [P, P])
        vx = sb("vx", [P, 2, 8, QUADS, VCOLS])
        qbd = sb("qbd", [P, 2, 8, QUADS, 64])
        mx = sb("mx", [P, 2, 32], BF16)

        def v(name, n=1):
            k = VEC.index(name)
            return vec[:, k:k + n]

        def wmat(name):
            return wm[:, WMATS.index(name), :]

        def cmat(name):
            return cm[:, CMATS.index(name), :]

        PAR = ["bq_s", "bk_lo", "bk_hi", "s1", "B1", "cb", "s2", "B2", "r1", "r2"]

        def par_(name):
            k = PAR.index(name)
            return par[:, k:k + 1]

        stack_b = ExitStack()
        xg = sb("xg", [P, 2, 512], F32, stack_b)
        lnst = sb("lnst", [P, 2, 4, 6], F32, stack_b)
        lnmv = sb("lnmv", [P, 2, 4, 2], F32, stack_b)
        lnve = sb("lnve", [P, 2, 4], F32, stack_b)
        lnrs = sb("lnrs", [P, 2, 4], F32, stack_b)
        xc = sb("xc", [P, 2, 512], F32, stack_b)
        xn = sb("xn", [P, 2, 512], F32, stack_b)
        kx = sb("kx", [P, 2, 8, 2, 64], F32, stack_b)
        q16 = sb("q16", [P, 2, 8, QUADS, 64], BF16, stack_b)
        k16 = sb("k16", [P, 2, 8, 2, 64], BF16, stack_b)
        mt16 = sb("mt16", [32, 2, P], BF16, stack_b)
        prob = sb("prob", [P, 8, QUADS, 64], F32, stack_b)
        rden = sb("rden", [P, 2, 4, 8], F32, stack_b)
        oh = sb("oh", [P, 2, 512], F32, stack_b)
        ot = sb("ot", [P, 2, 512], F32, stack_b)
        ob = sb("ob", [P, 2, 512], F32, stack_b)
        stack_b.close()
        stack_c = ctx.enter_context(ExitStack())
        qimg = sb("qimg", [P, (H + 2) * QW], F32, stack_c)
        tst = sb("tst", [P, 2, STRIP], F32, stack_c)
        kv = sb("kv", [P, 2, 2, 2, P], F32, stack_c)
        krel = sb("krel", [P, 2, 2, P], F32, stack_c)
        tb = sb("tb", [P, BLOCK], F32, stack_c)
        zb = sb("zb", [P, BLOCK], F32, stack_c)
        t1 = sb("t1", [P, 2, BLOCK], F32, stack_c)
        hb = sb("hb", [P, NF, BLOCK], F32, stack_c)
        sel_f = hb[0:32, :, :].rearrange("p a b -> p (a b)")[:, 0:16 * P]
        z2 = sb("z2", [P, BLOCK], F32, stack_c)
        z3 = sb("z3", [P, BLOCK], F32, stack_c)
        yb = sb("yb", [P, 2, BLOCK], F32, stack_c)

        bank = [ctx.enter_context(nc.psum_tensor(f"bank{n}", [P, 512], F32)) for n in range(8)]

        consts_loaded = sem("consts_loaded")
        x_loaded = sem("x_loaded")
        ones_set = sem("ones_set")
        waits_passed = sem("waits_passed")
        consts_cast = sem("consts_cast")
        par_sq = sem("par_sq")
        par_chain = sem("par_chain")
        par_ready = sem("par_ready")
        cb_mm = sem("cb_mm")
        gst_ready = sem("gst_ready")
        gmv_ready = sem("gmv_ready")
        gmean_mm = sem("gmean_mm")
        gdev1 = sem("gdev1")
        gdev_ready = sem("gdev_ready")
        gvar_mm = sem("gvar_mm")
        gvar_ready = sem("gvar_ready")
        grs_ready = sem("grs_ready")
        gcoef_ready = sem("gcoef_ready")
        xg_ready = sem("xg_ready")
        xt_mm = sem("xt_mm")
        lnst_ready = sem("lnst_ready")
        lnmv_ready = sem("lnmv_ready")
        lnve_ready = sem("lnve_ready")
        lnrs_ready = sem("lnrs_ready")
        xc_ready = sem("xc_ready")
        xnt_mm = sem("xnt_mm")
        xn_ready = sem("xn_ready")
        q_mm = sem("q_mm")
        q_ready = sem("q_ready")
        k_mm = sem("k_mm")
        k_ready = sem("k_ready")
        v_mm = sem("v_mm")
        v_ready = sem("v_ready")
        qk16_ready = sem("qk16_ready")
        smax_mm = sem("smax_mm")
        max_ready = sem("max_ready")
        mt_mm = sem("mt_mm")
        mt_ready = sem("mt_ready")
        st_mm = sem("st_mm")
        prob_ready = sem("prob_ready")
        pv_mm = sem("pv_mm")
        rden_ready = sem("rden_ready")
        oh_ready = sem("oh_ready")
        ot_mm = sem("ot_mm")
        ot_ready = sem("ot_ready")
        out_mm = sem("out_mm")
        ob_ready = sem("ob_ready")
        x1_ready = sem("x1_ready")
        pad_ready = sem("pad_ready")
        tst_ready = sem("tst_ready")
        lq_mm = sem("lq_mm")
        lq_ready = sem("lq_ready")
        kv_mm = sem("kv_mm")
        kv_ready = sem("kv_ready")
        krel_ready = sem("krel_ready")
        ctx_mm = sem("ctx_mm")
        ctxt_ready = sem("ctxt_ready")
        mtap_mm = sem("mtap_mm")
        mtap_ready = sem("mtap_ready")
        tb_ready = sem("tb_ready")
        conv_mm = sem("conv_mm")
        zb_ready = sem("zb_ready")
        t1_ready = sem("t1_ready")
        h_mm = sem("h_mm")
        h_ready = sem("h_ready")
        ff_mm = sem("ff_mm")
        z2_ready = sem("z2_ready")
        t2_ready = sem("t2_ready")
        y_ready = sem("y_ready")
        y_stored = [sem(f"y_stored{n}") for n in range(2)]

        NCONST = 8

        def windows(s, gg):
            w0, n = 2 * GROUP_FIRST[gg], 2 * GROUP_PAIRS[gg]
            a = ximg[:, bass.ds(s * STRIP, STRIP)]
            return a.rearrange("p (r w c) -> p w r c", r=WIN, w=W // WIN)[:, w0:w0 + n]

        def by_window(t, gg):
            n = 2 * GROUP_PAIRS[gg]
            return t[:, 0:64 * n].rearrange("p (w r c) -> p w r c", r=WIN, c=WIN)

        def group_loop(eng, i, step, prologue, epilogue):
            prologue(i * GROUPS)

            def strip(s, g0):
                for gg in range(2):
                    def near(k, g=g0 + gg if g0 is not None else None):
                        return g is None or 0 <= g + k < GROUPS
                    step(i * GROUPS + s * 2 + gg, s, gg, near)
            strip(0, 0)
            with eng.Fori(1, STRIPS - 1) as s:
                strip(s, None)
            strip(STRIPS - 1, GROUPS - 2)
            epilogue(i * GROUPS)

        def block_loop(eng, i, step):
            def strip(s):
                for bb in range(2):
                    step(i * BLOCKS + s * 2 + bb, s, s * 2 + bb, bb,
                         isinstance(s, int) and s == STRIPS - 1 and bb == 1)
            strip(0)
            with eng.Fori(1, STRIPS - 1) as s:
                strip(s)
            strip(STRIPS - 1)

        def hold(eng):
            eng.sem_inc(waits_passed, 1)

        block = ctx.enter_context(nc.Block())

        @block.sync
        def _(sp):
            for dst, src in ((vec, vec_d), (fc1b, fc1b_d), (dw, dw_d), (wm, wm_d), (cm, cm_d),
                             (w1, w1_d), (w2, w2_d), (sel_f, sel_d)):
                sp.dma_start(dst[:] if dst is not sel_f else sel_f, src).then_inc(consts_loaded, 16)
            for s in range(STRIPS):
                sp.dma_start(ximg[:, s * STRIP:(s + 1) * STRIP],
                             x_d[0, :, s * STRIP:(s + 1) * STRIP]).then_inc(x_loaded, 16)

            def store(i, b, bb, B):
                sp.wait_ge(y_ready, B + 1)
                sp.dma_start(out_d[bass.ds(i, 1), :, bass.ds(b * BLOCK, BLOCK)].rearrange("a p n -> p (a n)"),
                             yb[:, bb, :]).then_inc(y_stored[bb], 16)

            with sp.Fori(0, NIMG - 1) as i:
                def strip(s, last):
                    for bb in range(2):
                        store(i, s * 2 + bb, bb, i * BLOCKS + s * 2 + bb)
                    if last:
                        for bb in range(2):
                            sp.wait_ge(y_stored[bb], (i + 1) * (16 * STRIPS))
                    sp.dma_start(ximg[:, bass.ds(s * STRIP, STRIP)],
                                 x_d[bass.ds(i + 1, 1), :, bass.ds(s * STRIP, STRIP)]
                                 .rearrange("a p n -> p (a n)")).then_inc(x_loaded, 16)

                with sp.Fori(0, STRIPS - 1) as s:
                    strip(s, False)
                strip(STRIPS - 1, True)
            with sp.Fori(0, STRIPS) as s:
                for bb in range(2):
                    store(NIMG - 1, s * 2 + bb, bb, (NIMG - 1) * BLOCKS + s * 2 + bb)
            for bb in range(2):
                sp.wait_ge(y_stored[bb], 16 * NIMG * STRIPS)

        @block.gpsimd
        def _(pool):
            g = nc.gpsimd
            g.memset(neghalf[:], -0.5).then_inc(ones_set, 1)
            g.memset(vx[:], 0.0).then_inc(ones_set, 1)
            g.memset(mx[:], 0.0).then_inc(ones_set, 1)
            g.memset(qbd[:], 0.0).then_inc(ones_set, 1)
            pool.wait_ge(ones_set, 4)
            pool.wait_ge(par_sq, 2)
            g.tensor_tensor(par_("r1"), par_("s1"), neghalf[:, 0:1], ALU.pow).then_inc(par_chain, 1)
            g.tensor_tensor(par_("r2"), par_("s2"), neghalf[:, 0:1], ALU.pow).then_inc(par_chain, 1)

            def gn_coef(n):
                pool.wait_ge(gvar_ready, n + 1)
                hold(pool)
                g.tensor_tensor(gcoef[:, 0:1], gdev[:, 1:2], neghalf[:, 0:1], ALU.pow).then_inc(grs_ready, 1)
                pool.wait_ge(grs_ready, n + 1)
                hold(pool)
                g.tensor_scalar(gcoef[:, 1:2], gmv[:, 0:1], -1.0, gcoef[:, 0:1], ALU.mult, ALU.mult)\
                    .then_inc(gcoef_ready, 1)

            def ln_rstd(G, gg):
                n = GROUP_PAIRS[gg]
                pool.wait_ge(lnmv_ready, G + 1)
                hold(pool)
                g.tensor_scalar_add(lnve[:, gg, 0:n], lnmv[:, gg, 0:n, 1], LN_EPS).then_inc(lnve_ready, 1)
                pool.wait_ge(lnve_ready, G + 1)
                g.tensor_tensor(lnrs[:, gg, 0:n], lnve[:, gg, 0:n], neghalf[:, 0:n], ALU.pow)\
                    .then_inc(lnrs_ready, 1)

            def prologue(G):
                ln_rstd(G, 0)
                ln_rstd(G + 1, 1)

            def residual(G, s, gg):
                pool.wait_ge(ob_ready, G + 1)
                hold(pool)
                xw = windows(s, gg)
                g.tensor_tensor(xw, xw, by_window(ob[:, gg, :], gg), ALU.add).then_inc(x1_ready, 1)

            def step(G, s, gg, near):
                if near(-2):
                    residual(G - 2, s - 1, gg)
                if near(2):
                    ln_rstd(G + 2, gg)

            def epilogue(G0):
                for gg in range(2):
                    residual(G0 + GROUPS - 2 + gg, STRIPS - 1, gg)

            with pool.Fori(0, NIMG) as i:
                gn_coef(i * 2)
                group_loop(pool, i, step, prologue, epilogue)
                pool.wait_ge(x1_ready, (i + 1) * GROUPS)
                hold(pool)
                qv = qimg[:].rearrange("p (r c) -> p r c", c=QW)
                g.memset(qv[:, 0:1, :], 0.0)
                g.memset(qv[:, H + 1:H + 2, :], 0.0)
                g.memset(qv[:, 1:H + 1, 0:1], 0.0)
                g.memset(qv[:, 1:H + 1, QW - 1:QW], 0.0).then_inc(pad_ready, 1)
                gn_coef(i * 2 + 1)

        @block.scalar
        def _(act):
            a = nc.scalar
            act.wait_ge(par_ready, 1)

            def xn_evac(G, gg):
                n = P * GROUP_PAIRS[gg]
                act.wait_ge(xnt_mm, G + 1)
                a.activation(xn[:, gg, 0:n], bank[5][:, 0:n], ACT.Identity, bias=v("beta"),
                             scale=v("gamma")).then_inc(xn_ready, 1)

            def qk_evac(G, gg):
                n = P * GROUP_PAIRS[gg]
                act.wait_ge(q_mm, G + 1)
                for j in range(QUADS):
                    r = slice(32 * j, 32 * j + 32)
                    m = a.activation(qbd[r, gg, 0:n // 64, j, :],
                                     bank[4][r, 0:n].rearrange("p (w q) -> p w q", q=64), ACT.Identity,
                                     bias=par_("bq_s")[r], scale=float(HD) ** -0.5)
                m.then_inc(q_ready, 1)
                act.wait_ge(k_mm, G + 1)
                kp = bank[5][:, 0:n].rearrange("p (w k) -> p w k", k=64)
                a.activation(kx[:, gg, 0:n // 64, 0, :], kp, ACT.Identity, bias=par_("bk_lo"),
                             scale=v("mask_lo"))
                a.activation(kx[:, gg, 0:n // 64, 1, :], kp, ACT.Identity, bias=par_("bk_hi"),
                             scale=v("mask_hi")).then_inc(k_ready, 1)

            def exps(G, gg):
                for b in range(GROUP_PAIRS[gg]):
                    if b % 2 == 0:
                        act.wait_ge(st_mm, G * 2 + 1 + b // 2)
                    m = a.activation(prob[:, 2 * b:2 * b + 2].rearrange("p w j q -> p (w j q)"), bank[b][:],
                                     ACT.Exp)
                m.then_inc(prob_ready, 1)

            def ot_evac(G, gg):
                n = P * GROUP_PAIRS[gg]
                act.wait_ge(ot_mm, G + 1)
                a.activation(ot[:, gg, 0:n], bank[4][:, 0:n], ACT.Identity, bias=v("bv")).then_inc(ot_ready, 1)

            def ob_evac(G, gg):
                n = P * GROUP_PAIRS[gg]
                act.wait_ge(out_mm, G + 1)
                a.activation(ob[:, gg, 0:n], bank[5][:, 0:n], ACT.Identity, bias=v("bout"))\
                    .then_inc(ob_ready, 1)

            def prologue(G):
                xn_evac(G, 0)
                qk_evac(G, 0)
                xn_evac(G + 1, 1)

            def step(G, s, gg, near):
                if near(-2):
                    act.wait_ge(lnrs_ready, G + 1)
                    ob_evac(G - 2, gg)
                if near(1):
                    qk_evac(G + 1, 1 - gg)
                exps(G, gg)
                if near(2):
                    xn_evac(G + 2, gg)
                if near(-1):
                    ot_evac(G - 1, 1 - gg)

            def epilogue(G0):
                act.wait_ge(x1_ready, G0 + GROUPS - 2)
                ob_evac(G0 + GROUPS - 2, 0)
                ot_evac(G0 + GROUPS - 1, 1)
                ob_evac(G0 + GROUPS - 1, 1)

            with act.Fori(0, NIMG) as i:
                group_loop(act, i, step, prologue, epilogue)

                act.wait_ge(pad_ready, i + 1)

                def krel_evac(K, cc, n):
                    act.wait_ge(kv_ready, K + 1)
                    a.activation(krel[:, cc % 2, 0:n, :], kv[:, cc % 2, 0:n, 0, :], ACT.Relu)\
                        .then_inc(krel_ready, 1)

                def strip_c(s, first):
                    for bb in range(2):
                        B = i * BLOCKS + s * 2 + bb
                        act.wait_ge(lq_mm, B + 1)
                        rows = qimg[:, bass.ds((s * 2 + bb) * (BLOCK_ROWS * QW) + QW, BLOCK_ROWS * QW)]
                        a.activation(rows.rearrange("p (r c) -> p r c", c=QW)[:, :, 1:W + 1],
                                     bank[4 + bb][:, 0:BLOCK].rearrange("p (r c) -> p r c", c=W),
                                     ACT.Relu, bias=v("blq")).then_inc(lq_ready, 1)
                    for cc, (_, n) in enumerate(KV_CHUNKS):
                        K = (i * STRIPS + s) * len(KV_CHUNKS) + cc
                        if not (first and cc < 2):
                            act.wait_ge(ctx_mm, K - 1)
                        krel_evac(K, cc, n)

                strip_c(0, True)
                with act.Fori(1, STRIPS) as s:
                    strip_c(s, False)

                act.wait_ge(mtap_mm, i + 1)
                for t in range(3):
                    m = a.activation(mtap[:, 3 * t:3 * t + 3, :],
                                     bank[t][:, 0:3 * P].rearrange("p (t o) -> p t o", o=P), ACT.Copy)
                m.then_inc(mtap_ready, 1)

                def step_d(B, s, b, bb, last):
                    for j in range(NF):
                        act.wait_ge(h_mm, B * NF + j + 1)
                        a.activation(hb[:, j, :], bank[j % 4][:, 0:BLOCK], ACT.Gelu,
                                     bias=fc1b[:, j:j + 1]).then_inc(h_ready, 1)

                block_loop(act, i, step_d)

        @block.vector
        def _(dve):
            d = nc.vector
            dve.wait_ge(consts_loaded, 16 * NCONST)
            d.tensor_copy(ident16[:], cmat("ident"))
            d.tensor_copy(sel16[:].rearrange("p a b -> p (a b)"), sel_f).then_inc(consts_cast, 1)
            for t in range(9):
                d.tensor_scalar(wp9[:, t, :], wmat("wproj"), dw[:, t:t + 1], None, ALU.mult)
            d.tensor_scalar(par_("bq_s"), v("bq"), float(HD) ** -0.5, None, ALU.mult)
            d.tensor_tensor(par_("bk_lo"), v("bk"), v("mask_lo"), ALU.mult)
            d.tensor_tensor(par_("bk_hi"), v("bk"), v("mask_hi"), ALU.mult)
            d.tensor_scalar(par_("s1"), v("v1"), BN_EPS, None, ALU.add).then_inc(par_sq, 1)
            d.tensor_scalar(par_("s2"), v("v2"), BN_EPS, None, ALU.add).then_inc(par_sq, 1)
            dve.wait_ge(ones_set, 4)
            for s in range(2):
                c = (HD + 1) * s + HD
                for b in range(2):
                    d.memset(vx[64 * s:64 * s + 64, b, :, :, c:c + 1], 1.0)
            dve.wait_ge(par_chain, 2)
            d.tensor_tensor(par_("r1"), par_("r1"), v("g1"), ALU.mult)
            d.tensor_tensor(par_("r2"), par_("r2"), v("g2"), ALU.mult).then_inc(par_chain, 1)
            dve.wait_ge(par_chain, 3)
            d.tensor_tensor(par_("B1"), v("m1"), par_("r1"), ALU.mult)
            d.tensor_tensor(par_("B2"), v("m2"), par_("r2"), ALU.mult)
            d.tensor_tensor(par_("s1"), par_("r1"), v("a1"), ALU.add)
            d.tensor_tensor(par_("s2"), par_("r2"), v("a2"), ALU.add).then_inc(par_chain, 1)
            dve.wait_ge(par_chain, 4)
            d.tensor_tensor(par_("B1"), v("b1"), par_("B1"), ALU.subtract)
            d.tensor_tensor(par_("B2"), v("b2"), par_("B2"), ALU.subtract)
            dve.wait_ge(cb_mm, 1)
            d.tensor_tensor(par_("cb"), bank[7][:, 0:1], v("bproj"), ALU.add).then_inc(par_ready, 1)
            dve.wait_ge(par_ready, 1)

            def group_norm(n):
                dve.wait_ge(gst_ready, n + 1)
                hold(dve)
                d.bn_aggr(mv[:], gstats[:]).then_inc(gmv_ready, 1)
                dve.wait_ge(gmean_mm, n + 1)
                d.tensor_copy(gmv[:], bank[7][:, 0:2]).then_inc(gdev1, 1)
                dve.wait_ge(gdev1, n * 2 + 1)
                d.tensor_tensor(gdev[:, 0:1], mv[:, 0:1], gmv[:, 0:1], ALU.subtract).then_inc(gdev1, 1)
                dve.wait_ge(gdev1, n * 2 + 2)
                d.tensor_tensor(gdev[:, 0:1], gdev[:, 0:1], gdev[:, 0:1], ALU.mult).then_inc(gdev_ready, 1)
                dve.wait_ge(gvar_mm, n + 1)
                d.scalar_tensor_tensor(gdev[:, 1:2], bank[7][:, 2:3], GN_EPS, gmv[:, 1:2], ALU.add,
                                       ALU.add).then_inc(gvar_ready, 1)

            def gn_apply(G, s, gg):
                d.tensor_scalar(by_window(xg[:, gg, :], gg), windows(s, gg), gcoef[:, 0:1],
                                gcoef[:, 1:2], ALU.mult, ALU.add).then_inc(xg_ready, 1)

            def ln_stats(G, gg):
                n = GROUP_PAIRS[gg]
                dve.wait_ge(xt_mm, G + 1)
                for t in range(n):
                    m = d.bn_stats(lnst[:, gg, t, :], bank[5][:, P * t:P * t + P])
                m.then_inc(lnst_ready, 1)
                dve.wait_ge(lnst_ready, G + 1)
                hold(dve)
                for t in range(n):
                    m = d.bn_aggr(lnmv[:, gg, t, :], lnst[:, gg, t, :])
                m.then_inc(lnmv_ready, 1)

            def ln_norm(G, gg):
                n = GROUP_PAIRS[gg]
                dve.wait_ge(lnrs_ready, G + 1)
                for t in range(n):
                    m = d.tensor_scalar(xc[:, gg, P * t:P * t + P], bank[5][:, P * t:P * t + P],
                                        lnmv[:, gg, t, 0:1], lnrs[:, gg, t:t + 1], ALU.subtract, ALU.mult)
                m.then_inc(xc_ready, 1)

            def v_evac(G, gg):
                n = GROUP_PAIRS[gg]
                dve.wait_ge(v_mm, G + 1)
                for w2 in range(2):
                    for s in range(2):
                        src = bank[4][64 * w2:64 * w2 + 64, 0:P * n]\
                            .rearrange("p (t j s d) -> p t j s d", j=QUADS, s=2, d=HD)[:, :, :, s, :]
                        dst = vx[64 * s:64 * s + 64, gg, w2:2 * n:2, :, (HD + 1) * s:(HD + 1) * s + HD]
                        m = d.tensor_copy(dst, src)
                m.then_inc(v_ready, 1)

            def cast_qk(G, gg):
                n = GROUP_PAIRS[gg]
                dve.wait_ge(q_ready, G + 1)
                d.tensor_copy(q16[:, gg, 0:2 * n], qbd[:, gg, 0:2 * n])
                dve.wait_ge(k_ready, G + 1)
                d.tensor_copy(k16[:, gg, 0:2 * n], kx[:, gg, 0:2 * n]).then_inc(qk16_ready, 1)

            def maxima(G, gg):
                dve.wait_ge(smax_mm, G + 1)
                for b in range(GROUP_PAIRS[gg]):
                    m = d.tensor_reduce(mx[:, gg, 8 * b:8 * b + 8],
                                        bank[b][:].rearrange("p (e k) -> p e k", k=64), AX.X, ALU.max)
                m.then_inc(max_ready, 1)

            def mt_evac(G, gg):
                dve.wait_ge(mt_mm, G + 1)
                d.tensor_copy(mt16[:, gg, :], bank[4][0:32, 0:64].bitcast(BF16)).then_inc(mt_ready, 1)

            def normalise(G, gg, h):
                k = min(2, GROUP_PAIRS[gg] - 2 * h)
                dve.wait_ge(pv_mm, G * 2 + 1 + h)
                src = bank[6 + h][:, 0:k * QUADS * VCOLS].rearrange("p (t e c) -> p t e c", e=8, c=HD + 1)
                d.reciprocal(rden[:, gg, 2 * h:2 * h + k, :], src[:, :, :, HD]).then_inc(rden_ready, 1)
                dve.wait_ge(rden_ready, G * 2 + 1 + h)
                r = rden[:, gg, 2 * h:2 * h + k, :].unsqueeze(3).to_broadcast([P, k, 8, HD])
                dst = oh[:, gg, 2 * P * h:2 * P * h + P * k].rearrange("p (t e c) -> p t e c", e=8, c=HD)
                d.tensor_tensor(dst, src[:, :, :, 0:HD], r, ALU.mult).then_inc(oh_ready, 1)

            def prologue(G):
                gn_apply(G, 0, 0)
                gn_apply(G + 1, 0, 1)
                ln_stats(G, 0)
                ln_norm(G, 0)
                ln_stats(G + 1, 1)
                cast_qk(G, 0)
                ln_norm(G + 1, 1)
                v_evac(G, 0)

            def strip_stats(s, G):
                dve.wait_ge(x1_ready, G)
                for h in range(2):
                    src = ximg[:, bass.ds(s * STRIP + h * BLOCK, BLOCK)]
                    m = d.bn_stats(gstats[:, bass.ds(s * 2 + h, 1), :].rearrange("p a c -> p (a c)"), src)
                return m

            def step(G, s, gg, near):
                if near(2):
                    gn_apply(G + 2, s + 1, gg)
                maxima(G, gg)
                if near(-1):
                    normalise(G - 1, 1 - gg, 0)
                mt_evac(G, gg)
                if near(-1):
                    normalise(G - 1, 1 - gg, 1)
                if near(2):
                    ln_stats(G + 2, gg)
                if near(1):
                    cast_qk(G + 1, 1 - gg)
                if near(2):
                    ln_norm(G + 2, gg)
                if near(1):
                    v_evac(G + 1, 1 - gg)
                if gg == 1 and near(-2):
                    strip_stats(s - 1, G - 1)

            def epilogue(G0):
                normalise(G0 + GROUPS - 1, 1, 0)
                normalise(G0 + GROUPS - 1, 1, 1)
                strip_stats(STRIPS - 1, G0 + GROUPS).then_inc(gst_ready, 1)

            with dve.Fori(0, NIMG) as i:
                dve.wait_ge(x_loaded, (i + 1) * (16 * STRIPS))
                hold(dve)
                with dve.Fori(0, GROUPS) as h:
                    d.bn_stats(gstats[:, bass.ds(h, 1), :].rearrange("p a c -> p (a c)"),
                               ximg[:, bass.ds(h * BLOCK, BLOCK)])
                d.engine_nop().then_inc(gst_ready, 1)
                group_norm(i * 2)
                dve.wait_ge(gcoef_ready, i * 2 + 1)
                hold(dve)
                group_loop(dve, i, step, prologue, epilogue)
                group_norm(i * 2 + 1)

                dve.wait_ge(gcoef_ready, i * 2 + 2)
                hold(dve)

                def norm_strip(s, sp):
                    d.tensor_scalar(tst[:, sp, :], ximg[:, bass.ds(s * STRIP, STRIP)], gcoef[:, 0:1],
                                    gcoef[:, 1:2], ALU.mult, ALU.add).then_inc(tst_ready, 1)

                def strip_c(s, first):
                    for cc, (_, n) in enumerate(KV_CHUNKS):
                        K = (i * STRIPS + s) * len(KV_CHUNKS) + cc
                        dve.wait_ge(kv_mm, K + 1)
                        if not (first and cc < 2):
                            dve.wait_ge(ctx_mm, K - 1)
                        src = bank[2 + cc % 2][:, 0:2 * P * n].rearrange("p (t c) -> p t c", c=2 * P)
                        bias = cm[:, CMATS.index("bias_lk"):CMATS.index("bias_lk") + 2, :]\
                            .rearrange("p (a b) c -> p a (b c)", a=1).to_broadcast([P, n, 2 * P])
                        d.tensor_tensor(kv[:, cc % 2, 0:n].rearrange("p t b c -> p t (b c)"), src, bias,
                                        ALU.add).then_inc(kv_ready, 1)

                norm_strip(0, 0)
                norm_strip(1, 1)
                strip_c(0, True)
                norm_strip(2, 0)
                strip_c(1, False)
                with dve.Fori(1, STRIPS // 2 - 1) as h:
                    for sp in range(2):
                        norm_strip(h * 2 + sp + 1, 1 - sp)
                        strip_c(h * 2 + sp, False)
                norm_strip(STRIPS - 1, 1)
                strip_c(STRIPS - 2, False)
                strip_c(STRIPS - 1, False)
                dve.wait_ge(ctx_mm, (i + 1) * (STRIPS * len(KV_CHUNKS)))
                d.tensor_tensor(ctxt[:], bank[6][:, 0:P], cmat("cmask"), ALU.mult).then_inc(ctxt_ready, 1)

                def mix(B, b, bb):
                    d.tensor_scalar(tb[:], ximg[:, bass.ds(b * BLOCK, BLOCK)], gcoef[:, 0:1],
                                    gcoef[:, 1:2], ALU.mult, ALU.add).then_inc(tb_ready, 1)
                    dve.wait_ge(tb_ready, B + 1)
                    dve.wait_ge(conv_mm, B + 1)
                    d.scalar_tensor_tensor(zb[:], bank[4 + bb][:, 0:BLOCK], par_("cb"), tb[:], ALU.add,
                                           ALU.add).then_inc(zb_ready, 1)
                    dve.wait_ge(zb_ready, B + 1)
                    d.tensor_scalar(t1[:, bb, :], zb[:], par_("s1"), par_("B1"), ALU.mult, ALU.add)\
                        .then_inc(t1_ready, 1)

                def step_d(B, s, b, bb, last):
                    if not last:
                        mix(B + 1, b + 1, 1 - bb)
                    dve.wait_ge(ff_mm, B + 1)
                    d.scalar_tensor_tensor(z2[:], bank[6 + bb][:, 0:BLOCK], v("bfc2"), t1[:, bb, :],
                                           ALU.add, ALU.add).then_inc(z2_ready, 1)
                    dve.wait_ge(z2_ready, B + 1)
                    d.tensor_scalar(z3[:], z2[:], par_("s2"), par_("B2"), ALU.mult, ALU.add)\
                        .then_inc(t2_ready, 1)
                    if not (isinstance(b, int) and b < 2):
                        dve.wait_ge(y_stored[bb], (i * STRIPS + s) * 16)
                    dve.wait_ge(t2_ready, B + 1)
                    d.tensor_tensor(yb[:, bb, :], z3[:], ximg[:, bass.ds(b * BLOCK, BLOCK)],
                                    ALU.add).then_inc(y_ready, 1)

                mix(i * BLOCKS, 0, 0)
                block_loop(dve, i, step_d)

        @block.tensor
        def _(pe):
            mm = nc.tensor.matmul
            tr = nc.tensor.transpose
            pe.wait_ge(consts_loaded, 16 * NCONST)
            pe.wait_ge(consts_cast, 1)
            mm(bank[7][:, 0:1], wmat("wproj"), v("dwb"), start=True, stop=True).then_inc(cb_mm, 1)

            def group_norm(n):
                pe.wait_ge(gmv_ready, n + 1)
                mm(bank[7][:, 0:2], cmat("gmat"), mv[:], start=True, stop=True).then_inc(gmean_mm, 1)
                pe.wait_ge(gdev_ready, n + 1)
                mm(bank[7][:, 2:3], cmat("gmat"), gdev[:, 0:1], start=True, stop=True).then_inc(gvar_mm, 1)

            def ln_transpose(G, gg):
                pe.wait_ge(xg_ready, G + 1)
                for t in range(GROUP_PAIRS[gg]):
                    m = tr(bank[5][:, P * t:P * t + P], xg[:, gg, P * t:P * t + P], cmat("ident"))
                m.then_inc(xt_mm, 1)

            def ln_back(G, gg):
                pe.wait_ge(xc_ready, G + 1)
                for t in range(GROUP_PAIRS[gg]):
                    m = tr(bank[5][:, P * t:P * t + P], xc[:, gg, P * t:P * t + P], cmat("ident"))
                m.then_inc(xnt_mm, 1)

            def project_q(G, gg):
                n = P * GROUP_PAIRS[gg]
                pe.wait_ge(xn_ready, G + 1)
                mm(bank[4][:, 0:n], wmat("wq"), xn[:, gg, 0:n], start=True, stop=True).then_inc(q_mm, 1)

            def project_k(G, gg):
                n = P * GROUP_PAIRS[gg]
                mm(bank[5][:, 0:n], wmat("wk"), xn[:, gg, 0:n], start=True, stop=True).then_inc(k_mm, 1)

            def project_v(G, gg):
                for t in range(GROUP_PAIRS[gg]):
                    m = mm(bank[4][:, P * t:P * t + P], xn[:, gg, P * t:P * t + P], wmat("wv"),
                           start=True, stop=True)
                m.then_inc(v_mm, 1)

            def score_rows(G, gg):
                pe.wait_ge(qk16_ready, G + 1)
                for w in range(2 * GROUP_PAIRS[gg]):
                    for jj in range(2):
                        c = 256 * (w % 2) + P * jj
                        m = mm(bank[w // 2][:, c:c + P],
                               q16[:, gg, w, 2 * jj:2 * jj + 2, :].rearrange("p j q -> p (j q)"),
                               k16[:, gg, w, :, :].rearrange("p s k -> p (s k)"), start=True, stop=True)
                m.then_inc(smax_mm, 1)

            def transpose_maxima(G, gg):
                pe.wait_ge(max_ready, G + 1)
                tr(bank[4][0:32, 0:64].bitcast(BF16), mx[:, gg, :], ident16[:]).then_inc(mt_mm, 1)

            def score_cols(G, gg, h):
                for w in range(4 * h, min(4 * h + 4, 2 * GROUP_PAIRS[gg])):
                    c = 256 * (w % 2)
                    for jj in range(2):
                        mm(bank[w // 2][:, c + P * jj:c + P * jj + P], sel16[:, 2 * w + jj, :], mt16[:, gg, :],
                           start=(jj == 0), stop=True, skip_group_check=True)
                    m = mm(bank[w // 2][:, c:c + 256], kx[:, gg, w, :, :].rearrange("p s k -> p (s k)"),
                           qbd[:, gg, w, :, :].rearrange("p j q -> p (j q)"), start=False, stop=True,
                           skip_group_check=True)
                m.then_inc(st_mm, 1)

            def attend(G, gg, h):
                for w in range(4 * h, min(4 * h + 4, 2 * GROUP_PAIRS[gg])):
                    t, w2 = w // 2, w % 2
                    for j in range(QUADS):
                        c = (t % 2) * QUADS * VCOLS + j * VCOLS
                        m = mm(bank[6 + h][64 * w2:64 * w2 + 64, c:c + VCOLS], prob[:, w, j, :],
                               vx[:, gg, w, j, :], start=True, stop=True)
                m.then_inc(pv_mm, 1)

            def out_transpose(G, gg):
                pe.wait_ge(oh_ready, G * 2 + 2)
                for t in range(GROUP_PAIRS[gg]):
                    m = tr(bank[4][:, P * t:P * t + P], oh[:, gg, P * t:P * t + P], cmat("ident"))
                m.then_inc(ot_mm, 1)

            def out_project(G, gg):
                n = P * GROUP_PAIRS[gg]
                pe.wait_ge(ot_ready, G + 1)
                mm(bank[5][:, 0:n], wmat("wout"), ot[:, gg, 0:n], start=True, stop=True).then_inc(out_mm, 1)

            def prologue(G):
                ln_transpose(G, 0)
                ln_back(G, 0)
                project_q(G, 0)
                project_k(G, 0)
                pe.wait_ge(k_ready, G + 1)
                project_v(G, 0)
                ln_transpose(G + 1, 1)
                ln_back(G + 1, 1)

            def step(G, s, gg, near):
                ng = 1 - gg
                if near(-1):
                    pe.wait_ge(prob_ready, G)
                score_rows(G, gg)
                if near(1):
                    pe.wait_ge(xn_ready, G + 2)
                if near(-2):
                    out_project(G - 2, gg)
                if near(1):
                    if not near(-2):
                        pe.wait_ge(v_ready, G + 1)
                    project_q(G + 1, ng)
                    if near(-2):
                        pe.wait_ge(ob_ready, G - 1)
                    project_k(G + 1, ng)
                if near(-1):
                    pe.wait_ge(prob_ready, G)
                    pe.wait_ge(v_ready, G)
                    if near(-2):
                        pe.wait_ge(oh_ready, G * 2 - 2)
                    attend(G - 1, ng, 0)
                if near(1):
                    pe.wait_ge(q_ready, G + 2)
                else:
                    pe.wait_ge(ot_ready, G - 1)
                transpose_maxima(G, gg)
                if near(-1):
                    attend(G - 1, ng, 1)
                if near(2):
                    pe.wait_ge(k_ready, G + 2)
                    ln_transpose(G + 2, gg)
                pe.wait_ge(mt_ready, G + 1)
                score_cols(G, gg, 0)
                if near(1):
                    project_v(G + 1, ng)
                score_cols(G, gg, 1)
                if near(2):
                    ln_back(G + 2, gg)
                if near(-1):
                    if near(1):
                        pe.wait_ge(v_ready, G + 2)
                    out_transpose(G - 1, ng)

            def epilogue(G0):
                G = G0 + GROUPS - 1
                out_project(G - 1, 0)
                pe.wait_ge(prob_ready, G + 1)
                attend(G, 1, 0)
                attend(G, 1, 1)
                out_transpose(G, 1)
                pe.wait_ge(ob_ready, G)
                out_project(G, 1)

            with pe.Fori(0, NIMG) as i:
                group_norm(i * 2)
                group_loop(pe, i, step, prologue, epilogue)
                group_norm(i * 2 + 1)
                pe.wait_ge(ob_ready, (i + 1) * GROUPS)

                def lq(s, sp, bb):
                    B = i * BLOCKS + s * 2 + bb
                    mm(bank[4 + bb][:, 0:BLOCK], wmat("lwq"), tst[:, sp, bb * BLOCK:(bb + 1) * BLOCK],
                       start=True, stop=True).then_inc(lq_mm, 1)

                def lkv(sp, cc):
                    t0, n = KV_CHUNKS[cc]
                    for t in range(n):
                        m = mm(bank[2 + cc % 2][:, 2 * P * t:2 * P * t + 2 * P],
                               tst[:, sp, P * (t0 + t):P * (t0 + t) + P],
                               wm[:, WMATS.index("lwk"):WMATS.index("lwk") + 2, :].rearrange("p a b -> p (a b)"),
                               start=True, stop=True)
                    m.then_inc(kv_mm, 1)

                def context(K, cc, first=False, last=False):
                    n = KV_CHUNKS[cc][1]
                    pe.wait_ge(krel_ready, K + 1)
                    for t in range(n):
                        m = mm(bank[6][:, 0:P], kv[:, cc % 2, t, 1, :], krel[:, cc % 2, t, :],
                               start=(first and t == 0), stop=(last and t == n - 1), skip_group_check=True)
                    m.then_inc(ctx_mm, 1)

                def strip_c(s, sp, first):
                    K0 = (i * STRIPS + s) * len(KV_CHUNKS)
                    pe.wait_ge(tst_ready, i * STRIPS + s + 1)
                    for bb in range(2):
                        if not first:
                            pe.wait_ge(lq_ready, i * BLOCKS + s * 2 + bb - 1)
                        lq(s, sp, bb)
                    for cc in range(len(KV_CHUNKS)):
                        if cc >= 2:
                            pe.wait_ge(kv_ready, K0 + cc - 1)
                        elif not first:
                            pe.wait_ge(kv_ready, K0 + cc - 1)
                        lkv(sp, cc)
                        if cc > 0:
                            context(K0 + cc - 1, cc - 1, first=(first and cc == 1))
                        elif not first:
                            context(K0 - 1, len(KV_CHUNKS) - 1)

                strip_c(0, 0, True)
                strip_c(1, 1, False)
                with pe.Fori(1, STRIPS // 2) as h:
                    for sp in range(2):
                        strip_c(h * 2 + sp, sp, False)
                context((i + 1) * (STRIPS * len(KV_CHUNKS)) - 1, len(KV_CHUNKS) - 1, last=True)

                pe.wait_ge(ctxt_ready, i + 1)
                for t in range(3):
                    m = mm(bank[t][:, 0:3 * P], ctxt[:], wp9[:, 3 * t:3 * t + 3, :].rearrange("p a b -> p (a b)"),
                           start=True, stop=True)
                m.then_inc(mtap_mm, 1)
                pe.wait_ge(lq_ready, (i + 1) * BLOCKS)
                pe.wait_ge(mtap_ready, i + 1)

                def conv(B, b, bb):
                    for t, (dy, dx) in enumerate(TAPS):
                        src = qimg[:, bass.ds(b * (BLOCK_ROWS * QW) + dy * QW, BLOCK_ROWS * QW)]\
                            .rearrange("p (r c) -> p r c", c=QW)[:, :, dx:dx + W]
                        m = mm(bank[4 + bb][:, 0:BLOCK], mtap[:, t, :], src, start=(t == 0), stop=(t == 8))
                    m.then_inc(conv_mm, 1)

                def fc1(B, bb, j):
                    pe.wait_ge(h_ready, B * NF + j - 3) if j >= 4 else None
                    mm(bank[j % 4][:, 0:BLOCK], w1[:, P * j:P * j + P], t1[:, bb, :], start=True,
                       stop=True).then_inc(h_mm, 1)

                def fc2(B, bb, j):
                    pe.wait_ge(h_ready, B * NF + j + 1)
                    m = mm(bank[6 + bb][:, 0:BLOCK], w2[:, j, :], hb[:, j, :], start=(j == 0),
                           stop=(j == NF - 1))
                    if j == NF - 1:
                        m.then_inc(ff_mm, 1)

                LAG = 3

                def step_d(B, s, b, bb, last):
                    pe.wait_ge(t1_ready, B + 1)
                    for j in range(NF):
                        fc1(B, bb, j)
                        if j >= LAG:
                            fc2(B, bb, j - LAG)
                    if not last:
                        conv(B + 1, b + 1, 1 - bb)
                    for j in range(NF - LAG, NF):
                        fc2(B, bb, j)

                conv(i * BLOCKS, 0, 0)
                block_loop(pe, i, step_d)


_HEAD_ORDER = np.concatenate([np.arange(HD) + HD * (j + 4 * s) for j in range(QUADS) for s in range(2)])


def _constants():
    eye = np.eye(P, dtype=np.float32)
    grp = np.arange(P) // (C // 32)
    gmat = (grp[:, None] == grp[None, :]).astype(np.float32) * np.float32(0.25)
    head = np.arange(P) // HD
    cmask = (head[:, None] == head[None, :]).astype(np.float32) * np.float32(HD ** -0.5)
    sel = np.zeros((32, 16, P), np.float32)
    for r in range(32):
        sel[r, r // 2, 64 * (r % 2):64 * (r % 2) + 64] = -1.0
    mask_lo = ((np.arange(P) // HD) % 2 == 0).astype(np.float32)
    return eye, gmat, cmask, sel, mask_lo, np.float32(1) - mask_lo


def kernel(**inputs):
    import concourse.bacc as _bacc
    from concourse.bass_utils import run_bass_kernel_spmd as _run

    a = {k: np.asarray(t) for k, t in inputs.items()}
    eye, gmat, cmask, sel, mask_lo, mask_hi = _constants()
    o = _HEAD_ORDER
    wqkv, bqkv = a["L0_conv_w_qkv"], a["L0_conv_b_qkv"]
    lw, lb = a["L1_conv_Wqkv"], a["L1_conv_bqkv"]
    col = {
        "gamma": a["L0_conv_ln_gamma"], "beta": a["L0_conv_ln_beta"], "bq": bqkv[0:C][o],
        "bk": bqkv[C:2 * C][o], "bout": a["L0_conv_b_out"], "dwb": a["L1_conv_dw_b"],
        "bproj": a["L1_conv_bproj"], "g1": a["L1_conv_bn1_g"], "b1": a["L1_conv_bn1_b"],
        "m1": a["L1_conv_bn1_m"], "v1": a["L1_conv_bn1_v"], "a1": np.broadcast_to(a["L1_conv_alpha1"], (C,)),
        "bfc2": a["L1_conv_bfc2"], "g2": a["L1_conv_bn2_g"], "b2": a["L1_conv_bn2_b"],
        "m2": a["L1_conv_bn2_m"], "v2": a["L1_conv_bn2_v"],
        "a2": np.broadcast_to(a["L1_conv_alpha2"], (C,)), "mask_lo": mask_lo, "mask_hi": mask_hi,
        "bv": bqkv[2 * C:][o], "blq": lb[0:C],
    }
    vec = np.stack([col[n] for n in VEC], axis=1)
    wmats = {
        "wq": wqkv[0:C][o].T, "wk": wqkv[C:2 * C][o].T, "wv": wqkv[2 * C:][o].T,
        "wout": a["L0_conv_w_out"][:, o].T, "lwq": lw[:, 0:C], "lwk": lw[:, C:2 * C],
        "lwv": lw[:, 2 * C:], "wproj": a["L1_conv_Wproj"],
    }
    cmats = {
        "ident": eye, "gmat": gmat, "cmask": cmask,
        "bias_lk": np.broadcast_to(lb[C:2 * C], (P, C)), "bias_lv": np.broadcast_to(lb[2 * C:], (P, C)),
    }
    arrays = {
        "x_in": a["x"].reshape(NIMG, C, HW),
        "vec_in": vec,
        "fc1b_in": a["L1_conv_bfc1"].reshape(NF, P).T,
        "dw_in": a["L1_conv_dw_w"].reshape(C, 9),
        "wm_in": np.stack([wmats[n] for n in WMATS], axis=1),
        "cm_in": np.stack([cmats[n] for n in CMATS], axis=1),
        "w1_in": a["L1_conv_Wfc1"],
        "w2_in": a["L1_conv_Wfc2"].reshape(NF, P, C).transpose(1, 0, 2),
        "sel_in": sel.reshape(32, 16 * P),
    }
    arrays = {k: np.ascontiguousarray(t) for k, t in arrays.items()}
    nc = _bacc.Bacc("TRN2", target_bir_lowering=False, num_devices=1)
    args = [nc.dram_tensor(k, t.shape, mybir.dt.from_np(t.dtype), kind="ExternalInput").ap()
            for k, t in arrays.items()]
    args.append(nc.dram_tensor("y_out", (NIMG, C, HW), F32, kind="ExternalOutput").ap())
    build(nc, *args)
    r = _run(nc, [arrays], core_ids=[0])
    return r.results[0]["y_out"].reshape(NIMG, C, H, W)
```

```python
from contextlib import ExitStack

import numpy as np
import concourse.bass as bass
from concourse import mybir

F32 = mybir.dt.float32
BF16 = mybir.dt.bfloat16
F32R = mybir.dt.float32r
ALU = mybir.AluOpType
ACT = mybir.ActivationFunctionType
AX = mybir.AxisListType

P = 128
NIMG, C, H, W = 4, 128, 112, 112
HW = H * W
WIN, NH, HD = 8, 8, 16
STRIP_ROWS = WIN
STRIPS = H // STRIP_ROWS
STRIP = STRIP_ROWS * W
GROUP_PAIRS = (4, 3)
GROUP_FIRST = (0, 4)
GROUPS = 2 * STRIPS
QUADS = 4
VCOLS = 2 * (HD + 1)
BLOCK_ROWS = 4
BLOCK = BLOCK_ROWS * W
BLOCKS = H // BLOCK_ROWS
CM = 1024
NF = CM // P
QUADS_D = BLOCKS // 4
SPLIT_J = (0, 2, 3, 5)
NS = len(SPLIT_J)
WHOLE_J = tuple(j for j in range(NF) if j not in SPLIT_J)
FC1_BANKS = 4
FC2_LAG = 4
CTX_LAG = 2
QW = W + 2
RING = 4 * BLOCK_ROWS + 2
KV_CHUNKS = ((0, 2), (2, 2), (4, 2), (6, 1))
TAPS = [(dy, dx) for dy in range(3) for dx in range(3)]
NTAP = len(TAPS)
GN_EPS, LN_EPS, BN_EPS = 1e-5, 1e-5, 1e-5

VEC = ["gamma", "beta", "bq", "bk", "bout", "dwb", "bproj", "g1", "b1", "m1", "v1", "a1", "bfc2",
       "g2", "b2", "m2", "v2", "a2", "mask_lo", "mask_hi", "bv", "blq"]
NVEC = len(VEC)
WMATS = ["wq", "wk", "wv", "wout", "lwq", "lwk", "lwv", "wproj"]
CMATS = ["ident", "gmat", "cmask", "bias_lk", "bias_lv"]


def build(nc, x_d, vec_d, fc1b_d, dw_d, wm_d, cm_d, w1_d, w2_d, sel_d, out_d):
    with ExitStack() as ctx:
        def sb(name, shape, dt=F32, stack=ctx):
            return stack.enter_context(nc.sbuf_tensor(name, shape, dt))

        def sem(name):
            return ctx.enter_context(nc.semaphore(name))

        ximg = sb("ximg", [P, HW])
        vec = sb("vec", [P, NVEC])
        fc1b = sb("fc1b", [P, NF])
        dw = sb("dw", [P, 9])
        wm = sb("wm", [P, len(WMATS), P])
        cm = sb("cm", [P, len(CMATS), P])
        w1s = [sb(f"w1_{n}", [P, CM], F32R) for n in ("hi", "lo")]
        w2 = sb("w2", [P, NF, P])
        w2s = [sb(f"w2_{n}", [P, NS, P], F32R) for n in ("hi", "lo")]
        lws = [sb(f"lw_{n}", [P, 4, P], F32R) for n in ("hi", "lo")]
        pws = [sb(f"pw_{n}", [P, 2, P], F32R) for n in ("hi", "lo")]
        ctxs = [sb(f"ctx_{n}", [P, P], F32R) for n in ("hi", "lo")]
        oring = sb("oring", [P, RING, QW])
        ident16 = sb("ident16", [P, P], BF16)
        sel16 = sb("sel16", [32, 16, P], BF16)
        neghalf = sb("neghalf", [P, 4])
        par = sb("par", [P, 16])
        gstats = sb("gstats", [P, GROUPS, 6])
        mv = sb("mv", [P, 2])
        gmv = sb("gmv", [P, 2])
        gdev = sb("gdev", [P, 2])
        gcoef = sb("gcoef", [P, 4])
        ctxm = sb("ctxm", [P, P])
        gpar = sb("gpar", [P, 2])
        vx = sb("vx", [P, 2, 8, QUADS, VCOLS])
        qbd = sb("qbd", [P, 2, 8, QUADS, 64])
        mx = sb("mx", [P, 2, 32], BF16)

        def v(name, n=1):
            k = VEC.index(name)
            return vec[:, k:k + n]

        def wmat(name):
            return wm[:, WMATS.index(name), :]

        def cmat(name):
            return cm[:, CMATS.index(name), :]

        PAR = ["bq_s", "bk_lo", "bk_hi", "s1", "B1", "cb", "s2", "B2", "r1", "r2", "K1", "K2"]

        def par_(name):
            k = PAR.index(name)
            return par[:, k:k + 1]

        stack_b = ExitStack()
        xg = sb("xg", [P, 2, 512], F32, stack_b)
        lnst = sb("lnst", [P, 2, 4, 6], F32, stack_b)
        lnmv = sb("lnmv", [P, 2, 4, 2], F32, stack_b)
        lnve = sb("lnve", [P, 2, 4], F32, stack_b)
        lnrs = sb("lnrs", [P, 2, 4], F32, stack_b)
        xc = sb("xc", [P, 2, 512], F32, stack_b)
        xn = sb("xn", [P, 2, 512], F32, stack_b)
        xns = [sb(f"xn_{n}", [P, 2, 512], F32R, stack_b) for n in ("hi", "lo")]
        kx = sb("kx", [P, 2, 8, 2, 64], F32, stack_b)
        q16 = sb("q16", [P, 2, 8, QUADS, 64], BF16, stack_b)
        k16 = sb("k16", [P, 2, 8, 2, 64], BF16, stack_b)
        mt16 = sb("mt16", [32, 2, P], BF16, stack_b)
        prob = sb("prob", [P, 8, QUADS, 64], F32, stack_b)
        rden = sb("rden", [P, 2, 4, 8], F32, stack_b)
        oh = sb("oh", [P, 2, 512], F32, stack_b)
        ot = sb("ot", [P, 2, 512], F32, stack_b)
        ob = sb("ob", [P, 2, 512], F32, stack_b)
        stack_b.close()
        stack_c = ExitStack()
        tfull = sb("tfull", [P, 2, STRIP], F32, stack_c)
        tsth = sb("tsth", [P, 2, STRIP], F32R, stack_c)
        tstl = sb("tstl", [P, 2, STRIP], F32R, stack_c)
        kv = sb("kv", [P, 4, 2, 2, P], F32, stack_c)
        krel = sb("krel", [P, 4, 2, P], F32, stack_c)
        stack_c.close()
        stack_s = ExitStack()
        w1f = sb("w1f", [P, CM], F32, stack_s)
        sel_f = sb("sel_f", [32, 16 * P], F32, stack_s)
        stack_s.close()
        tf = sb("tf", [P, 2, BLOCK])
        tbh = sb("tbh", [P, 2, BLOCK], F32R)
        tbl = sb("tbl", [P, 2, BLOCK], F32R)
        qf = sb("qf", [P, BLOCK])
        qh = sb("qh", [P, 2, BLOCK], F32R)
        ql = sb("ql", [P, 2, BLOCK], F32R)
        dwh = sb("dwh", [P, BLOCK], F32R)
        dwl = sb("dwl", [P, BLOCK], F32R)
        ub = sb("ub", [P, 2, BLOCK])
        t1 = sb("t1", [P, 2, BLOCK])
        t1h = sb("t1h", [P, 2, BLOCK], F32R)
        t1l = sb("t1l", [P, 2, BLOCK], F32R)
        wb = sb("wb", [P, 2, BLOCK])
        xw = sb("xw", [P, 2, BLOCK])
        hf = sb("hf", [P, 2, BLOCK])
        hw = sb("hw", [P, NF - NS, BLOCK])
        hh = sb("hh", [P, NS, BLOCK], F32R)
        hl = sb("hl", [P, NS, BLOCK], F32R)
        yb = sb("yb", [P, 2, BLOCK])

        bank = [ctx.enter_context(nc.psum_tensor(f"bank{n}", [P, 512], F32)) for n in range(8)]

        consts_loaded = sem("consts_loaded")
        x_loaded = [sem(f"x_loaded{n}") for n in range(2)]
        ones_set = sem("ones_set")
        waits_passed = sem("waits_passed")
        consts_cast = sem("consts_cast")
        par_sq = sem("par_sq")
        par_chain = sem("par_chain")
        par_ready = sem("par_ready")
        cb_mm = sem("cb_mm")
        gst_ready = sem("gst_ready")
        gmv_ready = sem("gmv_ready")
        gmean_mm = sem("gmean_mm")
        gdev1 = sem("gdev1")
        gdev_ready = sem("gdev_ready")
        gvar_mm = sem("gvar_mm")
        gvar_ready = sem("gvar_ready")
        grs_ready = sem("grs_ready")
        gcoef_ready = sem("gcoef_ready")
        xg_ready = sem("xg_ready")
        xt_mm = sem("xt_mm")
        lnst_ready = sem("lnst_ready")
        lnmv_ready = sem("lnmv_ready")
        lnve_ready = sem("lnve_ready")
        lnrs_ready = sem("lnrs_ready")
        xc_ready = sem("xc_ready")
        xnt_mm = sem("xnt_mm")
        xn_ready = sem("xn_ready")
        xnl_ready = sem("xnl_ready")
        q_mm = sem("q_mm")
        q_ready = sem("q_ready")
        k_mm = sem("k_mm")
        k_ready = sem("k_ready")
        v_mm = sem("v_mm")
        v_ready = sem("v_ready")
        q16_ready = sem("q16_ready")
        k16_ready = sem("k16_ready")
        smax_mm = sem("smax_mm")
        max_ready = sem("max_ready")
        mt_mm = sem("mt_mm")
        mt_ready = sem("mt_ready")
        st_mm = sem("st_mm")
        prob_ready = sem("prob_ready")
        pv_mm = sem("pv_mm")
        rden_ready = sem("rden_ready")
        oh_ready = sem("oh_ready")
        ot_mm = sem("ot_mm")
        ot_ready = sem("ot_ready")
        out_mm = sem("out_mm")
        ob_ready = sem("ob_ready")
        x1_ready = sem("x1_ready")
        pad_ready = sem("pad_ready")
        tfull_ready = sem("tfull_ready")
        tsth_ready = sem("tsth_ready")
        tstl_ready = sem("tstl_ready")
        tf_ready = sem("tf_ready")
        tbh_ready = sem("tbh_ready")
        tbl_ready = sem("tbl_ready")
        lq_mm = sem("lq_mm")
        qh_ready = sem("qh_ready")
        ql_ready = sem("ql_ready")
        weights_hi = sem("weights_hi")
        weights_lo = sem("weights_lo")
        kv_mm = sem("kv_mm")
        kv_ready = sem("kv_ready")
        krel_ready = sem("krel_ready")
        ctx_mm = sem("ctx_mm")
        ctxm_ready = sem("ctxm_ready")
        o_mm = sem("o_mm")
        o_ready = sem("o_ready")
        tap_ready = sem("tap_ready")
        dwh_ready = sem("dwh_ready")
        dwl_ready = sem("dwl_ready")
        proj_mm = sem("proj_mm")
        gpar_ready = sem("gpar_ready")
        u_ready = sem("u_ready")
        t1_ready = sem("t1_ready")
        t1h_ready = sem("t1h_ready")
        t1l_ready = sem("t1l_ready")
        wb_ready = sem("wb_ready")
        xw_ready = sem("xw_ready")
        h_mm = sem("h_mm")
        hf_ready = sem("hf_ready")
        hh_ready = sem("hh_ready")
        hl_ready = sem("hl_ready")
        ff_mm = sem("ff_mm")
        y_ready = sem("y_ready")
        y_stored = [sem(f"y_stored{n}") for n in range(2)]

        NCONST = 8

        def windows(s, gg):
            w0, n = 2 * GROUP_FIRST[gg], 2 * GROUP_PAIRS[gg]
            a = ximg[:, bass.ds(s * STRIP, STRIP)]
            return a.rearrange("p (r w c) -> p w r c", r=WIN, w=W // WIN)[:, w0:w0 + n]

        def by_window(t, gg):
            n = 2 * GROUP_PAIRS[gg]
            return t[:, 0:64 * n].rearrange("p (w r c) -> p w r c", r=WIN, c=WIN)

        def group_loop(eng, i, step, prologue, epilogue):
            prologue(i * GROUPS)

            def strip(s, g0):
                for gg in range(2):
                    def near(k, g=g0 + gg if g0 is not None else None):
                        return g is None or 0 <= g + k < GROUPS
                    step(i * GROUPS + s * 2 + gg, s, gg, near)
            strip(0, 0)
            with eng.Fori(1, STRIPS - 1) as s:
                strip(s, None)
            strip(STRIPS - 1, GROUPS - 2)
            epilogue(i * GROUPS)

        def block_loop(eng, i, step):
            def four(h, b0):
                for u in range(4):
                    def near(k, b=b0 + u if b0 is not None else None):
                        return b is None or 0 <= b + k < BLOCKS
                    step(i * BLOCKS + h * 4 + u, h * 2 + u // 2, h * 4 + u, u, near)
            four(0, 0)
            with eng.Fori(1, QUADS_D - 2) as h:
                four(h, None)
            four(QUADS_D - 2, BLOCKS - 8)
            four(QUADS_D - 1, BLOCKS - 4)

        def ring_rows(u):
            return slice(1 + BLOCK_ROWS * u, 1 + BLOCK_ROWS * (u + 1))

        def ring_copies(u, prev, after):
            return ([(RING - 1, 0)] if u == 0 and prev else []) + \
                   ([(0, BLOCK_ROWS - 1)] if u == 3 and after else [])

        def value_blocks(gg):
            n = GROUP_PAIRS[gg]
            for w2 in range(2):
                for s in range(2):
                    src = bank[4][64 * w2:64 * w2 + 64, 0:P * n]\
                        .rearrange("p (t j s d) -> p t j s d", j=QUADS, s=2, d=HD)[:, :, :, s, :]
                    yield vx[64 * s:64 * s + 64, gg, w2:2 * n:2, :, (HD + 1) * s:(HD + 1) * s + HD], src

        def hold(eng):
            eng.sem_inc(waits_passed, 1)

        block = ctx.enter_context(nc.Block())

        @block.sync
        def _(sp):
            for dst, src in ((vec, vec_d), (fc1b, fc1b_d), (dw, dw_d), (wm, wm_d), (cm, cm_d),
                             (w1f, w1_d), (w2, w2_d), (sel_f, sel_d)):
                sp.dma_start(dst[:], src).then_inc(consts_loaded, 16)
            for s in range(STRIPS):
                if s >= 2:
                    sp.wait_ge(x_loaded[s % 2], 16 * (s // 2))
                sp.dma_start(ximg[:, s * STRIP:(s + 1) * STRIP],
                             x_d[0, :, s * STRIP:(s + 1) * STRIP]).then_inc(x_loaded[s % 2], 16)

            def store(i, b, bb, B):
                sp.wait_ge(y_ready, B + 1)
                sp.dma_start(out_d[bass.ds(i, 1), :, bass.ds(b * BLOCK, BLOCK)].rearrange("a p n -> p (a n)"),
                             yb[:, bb, :]).then_inc(y_stored[bb], 16)

            with sp.Fori(0, NIMG - 1) as i:
                def strip(h, sp_, last):
                    s = h * 2 + sp_
                    for bb in range(2):
                        store(i, s * 2 + bb, bb, i * BLOCKS + s * 2 + bb)
                    sp.wait_ge(x_loaded[sp_], (i * (STRIPS // 2) + (STRIPS // 2) + h) * 16)
                    hold(sp)
                    if last:
                        for bb in range(2):
                            sp.wait_ge(y_stored[bb], (i + 1) * (16 * STRIPS))
                    sp.dma_start(ximg[:, bass.ds(s * STRIP, STRIP)],
                                 x_d[bass.ds(i + 1, 1), :, bass.ds(s * STRIP, STRIP)]
                                 .rearrange("a p n -> p (a n)")).then_inc(x_loaded[sp_], 16)

                with sp.Fori(0, STRIPS // 2 - 1) as h:
                    strip(h, 0, False)
                    strip(h, 1, False)
                strip(STRIPS // 2 - 1, 0, False)
                strip(STRIPS // 2 - 1, 1, True)
            with sp.Fori(0, STRIPS) as s:
                for bb in range(2):
                    store(NIMG - 1, s * 2 + bb, bb, (NIMG - 1) * BLOCKS + s * 2 + bb)
            for bb in range(2):
                sp.wait_ge(y_stored[bb], 16 * NIMG * STRIPS)

        @block.gpsimd
        def _(pool):
            g = nc.gpsimd
            g.memset(neghalf[:], -0.5).then_inc(ones_set, 1)
            g.memset(vx[:], 0.0).then_inc(ones_set, 1)
            g.memset(mx[:], 0.0).then_inc(ones_set, 1)
            g.memset(qbd[:], 0.0).then_inc(ones_set, 1)
            g.memset(oring[:], 0.0).then_inc(ones_set, 1)
            pool.wait_ge(ones_set, 5)
            pool.wait_ge(par_sq, 2)
            g.tensor_tensor(par_("r1"), par_("s1"), neghalf[:, 0:1], ALU.pow).then_inc(par_chain, 1)
            g.tensor_tensor(par_("r2"), par_("s2"), neghalf[:, 0:1], ALU.pow).then_inc(par_chain, 1)

            def gn_coef(n):
                pool.wait_ge(gvar_ready, n + 1)
                hold(pool)
                g.tensor_tensor(gcoef[:, 0:1], gdev[:, 1:2], neghalf[:, 0:1], ALU.pow).then_inc(grs_ready, 1)
                pool.wait_ge(grs_ready, n + 1)
                hold(pool)
                g.tensor_scalar(gcoef[:, 1:2], gmv[:, 0:1], -1.0, gcoef[:, 0:1], ALU.mult, ALU.mult)\
                    .then_inc(gcoef_ready, 1)

            def ln_rstd(G, gg):
                n = GROUP_PAIRS[gg]
                pool.wait_ge(lnmv_ready, G + 1)
                hold(pool)
                g.tensor_scalar_add(lnve[:, gg, 0:n], lnmv[:, gg, 0:n, 1], LN_EPS).then_inc(lnve_ready, 1)
                pool.wait_ge(lnve_ready, G + 1)
                g.tensor_tensor(lnrs[:, gg, 0:n], lnve[:, gg, 0:n], neghalf[:, 0:n], ALU.pow)\
                    .then_inc(lnrs_ready, 1)

            def xn_low(G, gg):
                n = P * GROUP_PAIRS[gg]
                pool.wait_ge(xn_ready, G + 1)
                g.tensor_tensor(xns[1][:, gg, 0:n], xn[:, gg, 0:n], xns[0][:, gg, 0:n].bitcast(F32),
                                ALU.subtract).then_inc(xnl_ready, 1)

            def prologue(G):
                ln_rstd(G, 0)
                xn_low(G, 0)
                ln_rstd(G + 1, 1)
                xn_low(G + 1, 1)

            def residual(G, s, gg):
                pool.wait_ge(ob_ready, G + 1)
                hold(pool)
                xw = windows(s, gg)
                g.tensor_tensor(xw, xw, by_window(ob[:, gg, :], gg), ALU.add).then_inc(x1_ready, 1)

            def step(G, s, gg, near):
                if near(-2):
                    residual(G - 2, s - 1, gg)
                if near(2):
                    ln_rstd(G + 2, gg)
                    xn_low(G + 2, gg)

            def epilogue(G0):
                for gg in range(2):
                    residual(G0 + GROUPS - 2 + gg, STRIPS - 1, gg)

            with pool.Fori(0, NIMG) as i:
                gn_coef(i * 2)
                group_loop(pool, i, step, prologue, epilogue)
                gn_coef(i * 2 + 1)

                with pool.Fori(0, STRIPS // 2) as h:
                    for sp in range(2):
                        pool.wait_ge(tsth_ready, i * STRIPS + h * 2 + sp + 1)
                        g.tensor_tensor(tstl[:, sp, :], tfull[:, sp, :], tsth[:, sp, :].bitcast(F32),
                                        ALU.subtract).then_inc(tstl_ready, 1)

                def residual_d(B, b, bb):
                    pool.wait_ge(wb_ready, B + 1)
                    hold(pool)
                    g.tensor_tensor(xw[:, bb, :], wb[:, bb, :], ximg[:, bass.ds(b * BLOCK, BLOCK)],
                                    ALU.add).then_inc(xw_ready, 1)

                def step_d(B, s, b, u, near):
                    if u == 0 and not near(4):
                        pool.wait_ge(tap_ready, (B + 1) * NTAP)
                        hold(pool)
                        g.memset(oring[:, 0, :], 0.0)
                        g.memset(oring[:, RING - 1, :], 0.0).then_inc(pad_ready, 1)
                    for k in range(NS):
                        pool.wait_ge(hh_ready, B * NS + k + 1)
                        g.tensor_tensor(hl[:, k, :], hf[:, k % 2, :], hh[:, k, :].bitcast(F32),
                                        ALU.subtract).then_inc(hl_ready, 1)
                    if near(1):
                        residual_d(B + 1, b + 1, (u + 1) % 2)

                residual_d(i * BLOCKS, 0, 0)
                block_loop(pool, i, step_d)

        @block.scalar
        def _(act):
            a = nc.scalar
            act.wait_ge(consts_loaded, 16 * NCONST)
            a.activation(w1s[0][:], w1f[:], ACT.Copy)
            for k, j in enumerate(SPLIT_J):
                a.activation(w2s[0][:, k, :], w2[:, j, :], ACT.Copy)
            a.activation(pws[0][:], wm[:, 0:2, :], ACT.Copy)
            a.activation(lws[0][:], wm[:, WMATS.index("lwq"):WMATS.index("lwq") + 4, :], ACT.Copy)\
                .then_inc(weights_hi, 1)
            act.wait_ge(par_ready, 1)

            def xn_evac(G, gg):
                n = P * GROUP_PAIRS[gg]
                act.wait_ge(xnt_mm, G + 1)
                a.activation(xn[:, gg, 0:n], bank[5][:, 0:n], ACT.Identity, bias=v("beta"),
                             scale=v("gamma"))
                a.activation(xns[0][:, gg, 0:n], bank[5][:, 0:n], ACT.Identity, bias=v("beta"),
                             scale=v("gamma")).then_inc(xn_ready, 1)

            def qk_evac(G, gg):
                n = P * GROUP_PAIRS[gg]
                act.wait_ge(k_mm, G + 1)
                kp = bank[5][:, 0:n].rearrange("p (w k) -> p w k", k=64)
                a.activation(kx[:, gg, 0:n // 64, 0, :], kp, ACT.Identity, bias=par_("bk_lo"),
                             scale=v("mask_lo"))
                a.activation(kx[:, gg, 0:n // 64, 1, :], kp, ACT.Identity, bias=par_("bk_hi"),
                             scale=v("mask_hi")).then_inc(k_ready, 1)
                act.wait_ge(q_mm, G + 1)
                for j in range(QUADS):
                    r = slice(32 * j, 32 * j + 32)
                    m = a.activation(qbd[r, gg, 0:n // 64, j, :],
                                     bank[4][r, 0:n].rearrange("p (w q) -> p w q", q=64), ACT.Identity,
                                     bias=par_("bq_s")[r], scale=float(HD) ** -0.5)
                m.then_inc(q_ready, 1)

            def v_evac(G, gg):
                act.wait_ge(v_mm, G + 1)
                for dst, src in value_blocks(gg):
                    m = a.activation(dst, src, ACT.Copy)
                m.then_inc(v_ready, 1)

            def exps(G, gg):
                for b in range(GROUP_PAIRS[gg]):
                    if b % 2 == 0:
                        act.wait_ge(st_mm, G * 2 + 1 + b // 2)
                    m = a.activation(prob[:, 2 * b:2 * b + 2].rearrange("p w j q -> p (w j q)"), bank[b][:],
                                     ACT.Exp)
                    if b == 1 or b == GROUP_PAIRS[gg] - 1:
                        m.then_inc(prob_ready, 1)

            def ot_evac(G, gg):
                n = P * GROUP_PAIRS[gg]
                act.wait_ge(ot_mm, G + 1)
                a.activation(ot[:, gg, 0:n], bank[4][:, 0:n], ACT.Identity, bias=v("bv")).then_inc(ot_ready, 1)

            def ob_evac(G, gg):
                n = P * GROUP_PAIRS[gg]
                act.wait_ge(out_mm, G + 1)
                a.activation(ob[:, gg, 0:n], bank[5][:, 0:n], ACT.Identity, bias=v("bout"))\
                    .then_inc(ob_ready, 1)

            def prologue(G):
                xn_evac(G, 0)
                qk_evac(G, 0)
                v_evac(G, 0)
                xn_evac(G + 1, 1)

            def step(G, s, gg, near):
                if near(-2):
                    ot_evac(G - 2, gg)
                    act.wait_ge(lnrs_ready, G + 1)
                    ob_evac(G - 2, gg)
                if near(1):
                    qk_evac(G + 1, 1 - gg)
                exps(G, gg)
                if near(1) and gg == 1:
                    v_evac(G + 1, 1 - gg)
                if near(2):
                    xn_evac(G + 2, gg)

            def epilogue(G0):
                ot_evac(G0 + GROUPS - 2, 0)
                act.wait_ge(x1_ready, G0 + GROUPS - 2)
                ob_evac(G0 + GROUPS - 2, 0)
                ot_evac(G0 + GROUPS - 1, 1)
                ob_evac(G0 + GROUPS - 1, 1)

            with act.Fori(0, NIMG) as i:
                group_loop(act, i, step, prologue, epilogue)

                def high_strip(s, sp):
                    act.wait_ge(tfull_ready, i * STRIPS + s + 1)
                    a.activation(tsth[:, sp, :], tfull[:, sp, :], ACT.Copy).then_inc(tsth_ready, 1)

                def strip_c(s):
                    for cc, (_, n) in enumerate(KV_CHUNKS):
                        K = (i * STRIPS + s) * len(KV_CHUNKS) + cc
                        act.wait_ge(kv_ready, K + 1)
                        a.activation(krel[:, cc, 0:n, :], kv[:, cc, 0:n, 0, :], ACT.Relu)\
                            .then_inc(krel_ready, 1)

                high_strip(0, 0)
                with act.Fori(0, STRIPS // 2 - 1) as h:
                    high_strip(h * 2 + 1, 1)
                    strip_c(h * 2)
                    high_strip(h * 2 + 2, 0)
                    strip_c(h * 2 + 1)
                high_strip(STRIPS - 1, 1)
                strip_c(STRIPS - 2)
                strip_c(STRIPS - 1)

                def tb_high(B, bb):
                    act.wait_ge(tf_ready, B + 1)
                    a.activation(tbh[:, bb, :], tf[:, bb, :], ACT.Copy).then_inc(tbh_ready, 1)

                def q_high(B, bb, prev=True, n=4):
                    act.wait_ge(lq_mm, B + 1)
                    if prev:
                        act.wait_ge(ql_ready, B)
                    a.activation(qf[:], bank[n][:, 0:BLOCK], ACT.Relu, bias=v("blq"))
                    a.activation(qh[:, bb, :], bank[n][:, 0:BLOCK], ACT.Relu, bias=v("blq"))\
                        .then_inc(qh_ready, 1)

                def o_read(B, u, prev=True, after=True, n=4):
                    act.wait_ge(o_mm, B + 1)
                    rows = bank[n][:, 0:BLOCK].rearrange("p (r c) -> p r c", c=W)
                    for ring, row in ring_copies(u, prev, after):
                        a.activation(oring[:, ring, 1:W + 1], rows[:, row, :], ACT.Copy)
                    a.activation(oring[:, ring_rows(u), 1:W + 1], rows, ACT.Copy).then_inc(o_ready, 1)

                def dw_high(B):
                    act.wait_ge(tap_ready, (B + 1) * NTAP)
                    a.activation(dwh[:], bank[5][:, 0:BLOCK], ACT.Copy).then_inc(dwh_ready, 1)

                def scaled_x(B, b, bb):
                    a.activation(ub[:, bb, :], ximg[:, bass.ds(b * BLOCK, BLOCK)], ACT.Identity,
                                 bias=gpar[:, 1:2], scale=gpar[:, 0:1]).then_inc(u_ready, 1)

                def t1_high(B, bb):
                    act.wait_ge(t1_ready, B + 1)
                    a.activation(t1h[:, bb, :], t1[:, bb, :], ACT.Copy).then_inc(t1h_ready, 1)
                    a.activation(wb[:, bb, :], t1[:, bb, :], ACT.Identity, bias=par_("K2"),
                                 scale=par_("s2")).then_inc(wb_ready, 1)

                def hidden(B, j):
                    H = B * NF + j
                    act.wait_ge(h_mm, H + 1)
                    if j not in SPLIT_J:
                        a.activation(hw[:, WHOLE_J.index(j), :], bank[j % FC1_BANKS][:, 0:BLOCK], ACT.Gelu,
                                     bias=fc1b[:, j:j + 1]).then_inc(hf_ready, 1)
                        return
                    k = SPLIT_J.index(j)
                    if k >= 2:
                        act.wait_ge(hl_ready, B * NS + k - 1)
                    a.activation(hf[:, k % 2, :], bank[j % FC1_BANKS][:, 0:BLOCK], ACT.Gelu,
                                 bias=fc1b[:, j:j + 1]).then_inc(hf_ready, 1)
                    act.wait_ge(hf_ready, H + 1)
                    a.activation(hh[:, k, :], hf[:, k % 2, :], ACT.Copy).then_inc(hh_ready, 1)

                def step_d(B, s, b, u, near):
                    if near(1):
                        scaled_x(B + 1, b + 1, (u + 1) % 2)
                        dw_high(B + 1)
                    for j in range(NF):
                        hidden(B, j)
                        if j == 1 and near(4):
                            q_high(B + 4, u % 2)
                        if j == 2 and near(5):
                            tb_high(B + 5, (u + 1) % 2)
                        if j == 5 and near(1):
                            t1_high(B + 1, (u + 1) % 2)
                    if near(4):
                        o_read(B + 4, u, after=near(5))

                B0 = i * BLOCKS
                act.wait_ge(gpar_ready, i + 1)
                tb_high(B0, 0)
                tb_high(B0 + 1, 1)
                q_high(B0, 0, prev=False, n=0)
                tb_high(B0 + 2, 0)
                q_high(B0 + 1, 1, n=1)
                for k in range(2, 4):
                    o_read(B0 + k - 2, k - 2, prev=False, n=4 + k)
                    tb_high(B0 + k + 1, (k + 1) % 2)
                    q_high(B0 + k, k % 2, n=k)
                o_read(B0 + 2, 2, n=6)
                scaled_x(B0, 0, 0)
                dw_high(B0)
                o_read(B0 + 3, 3, n=7)
                t1_high(B0, 0)
                block_loop(act, i, step_d)

        @block.vector
        def _(dve):
            d = nc.vector
            dve.wait_ge(consts_loaded, 16 * NCONST)
            d.tensor_copy(ident16[:], cmat("ident"))
            d.tensor_copy(sel16[:].rearrange("p a b -> p (a b)"), sel_f[:]).then_inc(consts_cast, 1)
            d.tensor_scalar(par_("bq_s"), v("bq"), float(HD) ** -0.5, None, ALU.mult)
            d.tensor_tensor(par_("bk_lo"), v("bk"), v("mask_lo"), ALU.mult)
            d.tensor_tensor(par_("bk_hi"), v("bk"), v("mask_hi"), ALU.mult)
            d.tensor_scalar(par_("s1"), v("v1"), BN_EPS, None, ALU.add).then_inc(par_sq, 1)
            d.tensor_scalar(par_("s2"), v("v2"), BN_EPS, None, ALU.add).then_inc(par_sq, 1)
            dve.wait_ge(ones_set, 5)
            for s in range(2):
                c = (HD + 1) * s + HD
                for b in range(2):
                    d.memset(vx[64 * s:64 * s + 64, b, :, :, c:c + 1], 1.0)
            dve.wait_ge(par_chain, 2)
            d.tensor_tensor(par_("r1"), par_("r1"), v("g1"), ALU.mult)
            d.tensor_tensor(par_("r2"), par_("r2"), v("g2"), ALU.mult).then_inc(par_chain, 1)
            dve.wait_ge(par_chain, 3)
            d.tensor_tensor(par_("B1"), v("m1"), par_("r1"), ALU.mult)
            d.tensor_tensor(par_("B2"), v("m2"), par_("r2"), ALU.mult)
            d.tensor_tensor(par_("s1"), par_("r1"), v("a1"), ALU.add)
            d.tensor_tensor(par_("s2"), par_("r2"), v("a2"), ALU.add).then_inc(par_chain, 1)
            dve.wait_ge(par_chain, 4)
            d.tensor_tensor(par_("B1"), v("b1"), par_("B1"), ALU.subtract)
            d.tensor_tensor(par_("B2"), v("b2"), par_("B2"), ALU.subtract)
            dve.wait_ge(cb_mm, 1)
            d.tensor_tensor(par_("cb"), bank[7][:, 0:1], v("bproj"), ALU.add).then_inc(par_chain, 1)
            dve.wait_ge(par_chain, 5)
            d.scalar_tensor_tensor(par_("K1"), par_("cb"), par_("s1"), par_("B1"), ALU.mult, ALU.add)
            d.scalar_tensor_tensor(par_("K2"), v("bfc2"), par_("s2"), par_("B2"), ALU.mult, ALU.add)\
                .then_inc(par_ready, 1)
            dve.wait_ge(weights_hi, 1)
            d.tensor_tensor(w1s[1][:], w1f[:], w1s[0][:].bitcast(F32), ALU.subtract)
            for k, j in enumerate(SPLIT_J):
                d.tensor_tensor(w2s[1][:, k, :], w2[:, j, :], w2s[0][:, k, :].bitcast(F32), ALU.subtract)
            d.tensor_tensor(pws[1][:], wm[:, 0:2, :], pws[0][:].bitcast(F32), ALU.subtract)
            d.tensor_tensor(lws[1][:], wm[:, WMATS.index("lwq"):WMATS.index("lwq") + 4, :],
                            lws[0][:].bitcast(F32), ALU.subtract).then_inc(weights_lo, 1)
            dve.wait_ge(par_ready, 1)

            def group_norm(n):
                dve.wait_ge(gst_ready, n + 1)
                hold(dve)
                d.bn_aggr(mv[:], gstats[:]).then_inc(gmv_ready, 1)
                dve.wait_ge(gmean_mm, n + 1)
                d.tensor_copy(gmv[:], bank[7][:, 0:2]).then_inc(gdev1, 1)
                dve.wait_ge(gdev1, n * 2 + 1)
                d.tensor_tensor(gdev[:, 0:1], mv[:, 0:1], gmv[:, 0:1], ALU.subtract).then_inc(gdev1, 1)
                dve.wait_ge(gdev1, n * 2 + 2)
                d.tensor_tensor(gdev[:, 0:1], gdev[:, 0:1], gdev[:, 0:1], ALU.mult).then_inc(gdev_ready, 1)
                dve.wait_ge(gvar_mm, n + 1)
                d.scalar_tensor_tensor(gdev[:, 1:2], bank[7][:, 2:3], GN_EPS, gmv[:, 1:2], ALU.add,
                                       ALU.add).then_inc(gvar_ready, 1)

            def gn_apply(G, s, gg):
                d.tensor_scalar(by_window(xg[:, gg, :], gg), windows(s, gg), gcoef[:, 0:1],
                                gcoef[:, 1:2], ALU.mult, ALU.add).then_inc(xg_ready, 1)

            def ln_stats(G, gg):
                n = GROUP_PAIRS[gg]
                dve.wait_ge(xt_mm, G + 1)
                for t in range(n):
                    m = d.bn_stats(lnst[:, gg, t, :], bank[5][:, P * t:P * t + P])
                m.then_inc(lnst_ready, 1)
                dve.wait_ge(lnst_ready, G + 1)
                hold(dve)
                for t in range(n):
                    m = d.bn_aggr(lnmv[:, gg, t, :], lnst[:, gg, t, :])
                m.then_inc(lnmv_ready, 1)

            def ln_norm(G, gg):
                n = GROUP_PAIRS[gg]
                dve.wait_ge(lnrs_ready, G + 1)
                for t in range(n):
                    m = d.tensor_scalar(xc[:, gg, P * t:P * t + P], bank[5][:, P * t:P * t + P],
                                        lnmv[:, gg, t, 0:1], lnrs[:, gg, t:t + 1], ALU.subtract, ALU.mult)
                m.then_inc(xc_ready, 1)

            def v_evac(G, gg):
                dve.wait_ge(v_mm, G + 1)
                for dst, src in value_blocks(gg):
                    m = d.tensor_copy(dst, src)
                m.then_inc(v_ready, 1)

            def cast_k(G, gg):
                n = GROUP_PAIRS[gg]
                dve.wait_ge(k_ready, G + 1)
                d.tensor_copy(k16[:, gg, 0:2 * n], kx[:, gg, 0:2 * n]).then_inc(k16_ready, 1)

            def cast_q(G, gg):
                n = GROUP_PAIRS[gg]
                dve.wait_ge(q_ready, G + 1)
                d.tensor_copy(q16[:, gg, 0:2 * n], qbd[:, gg, 0:2 * n]).then_inc(q16_ready, 1)

            def maxima(G, gg):
                dve.wait_ge(smax_mm, G + 1)
                for b in range(GROUP_PAIRS[gg]):
                    m = d.tensor_reduce(mx[:, gg, 8 * b:8 * b + 8],
                                        bank[b][:].rearrange("p (e k) -> p e k", k=64), AX.X, ALU.max)
                m.then_inc(max_ready, 1)

            def mt_evac(G, gg):
                dve.wait_ge(mt_mm, G + 1)
                d.tensor_copy(mt16[:, gg, :], bank[7][0:32, 448:512].bitcast(BF16)).then_inc(mt_ready, 1)

            def normalise(G, gg, h):
                k = min(2, GROUP_PAIRS[gg] - 2 * h)
                dve.wait_ge(pv_mm, G * 2 + 1 + h)
                src = bank[6 + h][:, 0:k * QUADS * VCOLS].rearrange("p (t e c) -> p t e c", e=8, c=HD + 1)
                d.reciprocal(rden[:, gg, 2 * h:2 * h + k, :], src[:, :, :, HD]).then_inc(rden_ready, 1)
                dve.wait_ge(rden_ready, G * 2 + 1 + h)
                r = rden[:, gg, 2 * h:2 * h + k, :].unsqueeze(3).to_broadcast([P, k, 8, HD])
                dst = oh[:, gg, 2 * P * h:2 * P * h + P * k].rearrange("p (t e c) -> p t e c", e=8, c=HD)
                d.tensor_tensor(dst, src[:, :, :, 0:HD], r, ALU.mult).then_inc(oh_ready, 1)

            def prologue(G):
                gn_apply(G, 0, 0)
                gn_apply(G + 1, 0, 1)
                ln_stats(G, 0)
                ln_norm(G, 0)
                ln_stats(G + 1, 1)
                cast_k(G, 0)
                ln_norm(G + 1, 1)
                cast_q(G, 0)

            def strip_stats(s, G):
                dve.wait_ge(x1_ready, G)
                for h in range(2):
                    src = ximg[:, bass.ds(s * STRIP + h * BLOCK, BLOCK)]
                    m = d.bn_stats(gstats[:, bass.ds(s * 2 + h, 1), :].rearrange("p a c -> p (a c)"), src)
                return m

            def step(G, s, gg, near):
                maxima(G, gg)
                if near(2):
                    gn_apply(G + 2, s + 1, gg)
                if near(-1):
                    normalise(G - 1, 1 - gg, 0)
                    dve.wait_ge(mt_mm, G + 1)
                    normalise(G - 1, 1 - gg, 1)
                mt_evac(G, gg)
                if gg == 1 and near(-2):
                    strip_stats(s - 1, G - 1)
                if near(1):
                    cast_k(G + 1, 1 - gg)
                if near(2):
                    ln_stats(G + 2, gg)
                if near(1):
                    cast_q(G + 1, 1 - gg)
                if near(2):
                    ln_norm(G + 2, gg)
                if near(1) and gg == 0:
                    v_evac(G + 1, 1)

            def epilogue(G0):
                normalise(G0 + GROUPS - 1, 1, 0)
                normalise(G0 + GROUPS - 1, 1, 1)
                strip_stats(STRIPS - 1, G0 + GROUPS).then_inc(gst_ready, 1)

            def loaded_stats(s):
                for h in range(2):
                    src = ximg[:, bass.ds(s * STRIP + h * BLOCK, BLOCK)]
                    m = d.bn_stats(gstats[:, bass.ds(s * 2 + h, 1), :].rearrange("p a c -> p (a c)"), src)
                return m

            for s in range(STRIPS):
                dve.wait_ge(x_loaded[s % 2], 16 * (s // 2 + 1))
                m = loaded_stats(s)
            m.then_inc(gst_ready, 1)

            def image(i, next_image):
                group_norm(i * 2)
                dve.wait_ge(gcoef_ready, i * 2 + 1)
                hold(dve)
                group_loop(dve, i, step, prologue, epilogue)
                group_norm(i * 2 + 1)

                dve.wait_ge(gcoef_ready, i * 2 + 2)
                hold(dve)

                def norm_strip(s, sp, reuse=True):
                    if reuse:
                        dve.wait_ge(tstl_ready, i * STRIPS + s - 1)
                    d.tensor_scalar(tfull[:, sp, :], ximg[:, bass.ds(s * STRIP, STRIP)], gcoef[:, 0:1],
                                    gcoef[:, 1:2], ALU.mult, ALU.add).then_inc(tfull_ready, 1)

                def strip_c(s):
                    for cc, (_, n) in enumerate(KV_CHUNKS):
                        dve.wait_ge(kv_mm, (i * STRIPS + s) * len(KV_CHUNKS) + cc + 1)
                        src = bank[2 + cc][:, 0:2 * P * n].rearrange("p (t c) -> p t c", c=2 * P)
                        bias = cm[:, CMATS.index("bias_lk"):CMATS.index("bias_lk") + 2, :]\
                            .rearrange("p (a b) c -> p a (b c)", a=1).to_broadcast([P, n, 2 * P])
                        d.tensor_tensor(kv[:, cc, 0:n].rearrange("p t b c -> p t (b c)"), src, bias,
                                        ALU.add).then_inc(kv_ready, 1)

                norm_strip(0, 0, False)
                norm_strip(1, 1, False)
                with dve.Fori(0, STRIPS // 2 - 1) as h:
                    for sp in range(2):
                        strip_c(h * 2 + sp)
                        norm_strip(h * 2 + sp + 2, sp)
                strip_c(STRIPS - 2)
                strip_c(STRIPS - 1)

                def norm_block(B, b, bb):
                    d.tensor_scalar(tf[:, bb, :], ximg[:, bass.ds(b * BLOCK, BLOCK)], gcoef[:, 0:1],
                                    gcoef[:, 1:2], ALU.mult, ALU.add).then_inc(tf_ready, 1)

                def tb_low(B, bb):
                    dve.wait_ge(tbh_ready, B + 1)
                    d.tensor_tensor(tbl[:, bb, :], tf[:, bb, :], tbh[:, bb, :].bitcast(F32), ALU.subtract)\
                        .then_inc(tbl_ready, 1)

                def q_low(B, bb):
                    dve.wait_ge(qh_ready, B + 1)
                    d.tensor_tensor(ql[:, bb, :], qf[:], qh[:, bb, :].bitcast(F32), ALU.subtract)\
                        .then_inc(ql_ready, 1)

                def taps(B, u, k0, k1, last, first=False):
                    acc = bank[5][:, 0:BLOCK].rearrange("p (r c) -> p r c", c=W)
                    for k in range(k0, k1):
                        dy, dx = TAPS[k]
                        if k == 0:
                            if not first:
                                dve.wait_ge(dwl_ready, B)
                            dve.wait_ge(o_ready, B + 1 if last else B + 2)
                            if last:
                                dve.wait_ge(pad_ready, i + 1)
                        else:
                            dve.wait_ge(tap_ready, B * NTAP + k)
                        src = oring[:, BLOCK_ROWS * u + dy:BLOCK_ROWS * (u + 1) + dy, dx:dx + W]
                        if k == 0:
                            m = d.tensor_scalar(acc, src, dw[:, k:k + 1], None, ALU.mult)
                        else:
                            m = d.scalar_tensor_tensor(acc, src, dw[:, k:k + 1], acc, ALU.mult, ALU.add)
                        m.then_inc(tap_ready, 1)

                def dw_low(B):
                    dve.wait_ge(dwh_ready, B + 1)
                    d.tensor_tensor(dwl[:], bank[5][:, 0:BLOCK], dwh[:].bitcast(F32), ALU.subtract)\
                        .then_inc(dwl_ready, 1)

                def mix(B, bb):
                    dve.wait_ge(u_ready, B + 1)
                    dve.wait_ge(proj_mm, B + 1)
                    d.scalar_tensor_tensor(t1[:, bb, :], bank[4][:, 0:BLOCK], par_("s1"), ub[:, bb, :],
                                           ALU.mult, ALU.add).then_inc(t1_ready, 1)

                def t1_low(B, bb):
                    dve.wait_ge(t1h_ready, B + 1)
                    d.tensor_tensor(t1l[:, bb, :], t1[:, bb, :], t1h[:, bb, :].bitcast(F32),
                                    ALU.subtract).then_inc(t1l_ready, 1)

                def finish(B, s, bb, reuse):
                    if reuse:
                        dve.wait_ge(y_stored[bb], (i * STRIPS + s) * 16)
                    dve.wait_ge(xw_ready, B + 1)
                    dve.wait_ge(ff_mm, B + 1)
                    d.scalar_tensor_tensor(yb[:, bb, :], bank[6 + bb][:, 0:BLOCK], par_("s2"), xw[:, bb, :],
                                           ALU.mult, ALU.add).then_inc(y_ready, 1)

                def next_stats(s, sp):
                    dve.wait_ge(x_loaded[sp], (i + 1) * (16 * STRIPS // 2) + s * 8 + (16 - 8 * sp))
                    hold(dve)
                    return loaded_stats(s)

                def step_d(B, s, b, u, near):
                    if near(-1):
                        finish(B - 1, s - (u + 1) % 2, (u + 1) % 2, near(-3))
                    if near(1):
                        dw_low(B + 1)
                    if near(5):
                        norm_block(B + 5, b + 5, (u + 1) % 2)
                    if near(2):
                        taps(B + 2, (u + 2) % 4, 0, 3, not near(3))
                    if near(4):
                        q_low(B + 4, u % 2)
                    if near(2):
                        taps(B + 2, (u + 2) % 4, 3, 5, not near(3))
                    if near(1):
                        mix(B + 1, (u + 1) % 2)
                    if near(5):
                        tb_low(B + 5, (u + 1) % 2)
                    if near(2):
                        taps(B + 2, (u + 2) % 4, 5, 7, not near(3))
                    if near(1):
                        t1_low(B + 1, (u + 1) % 2)
                    if near(2):
                        taps(B + 2, (u + 2) % 4, 7, NTAP, not near(3))
                    if next_image and u % 2 == 1 and near(-4):
                        next_stats(s - 2, u // 2)

                B0 = i * BLOCKS
                d.tensor_scalar(gpar[:, 0:1], gcoef[:, 0:1], par_("s1"), None, ALU.mult)
                d.scalar_tensor_tensor(gpar[:, 1:2], gcoef[:, 1:2], par_("s1"), par_("K1"), ALU.mult,
                                       ALU.add).then_inc(gpar_ready, 1)
                dve.wait_ge(tstl_ready, (i + 1) * STRIPS)
                for b in range(2):
                    norm_block(B0 + b, b, b)
                    tb_low(B0 + b, b)
                dve.wait_ge(ctx_mm, (i + 1) * (STRIPS * len(KV_CHUNKS)))
                d.tensor_tensor(ctxm[:], bank[6][:, 0:P], cmat("cmask"), ALU.mult).then_inc(ctxm_ready, 1)
                dve.wait_ge(ctxm_ready, i * 3 + 1)
                d.tensor_copy(ctxs[0][:], ctxm[:]).then_inc(ctxm_ready, 1)
                dve.wait_ge(ctxm_ready, i * 3 + 2)
                d.tensor_tensor(ctxs[1][:], ctxm[:], ctxs[0][:].bitcast(F32), ALU.subtract)\
                    .then_inc(ctxm_ready, 1)
                q_low(B0, 0)
                norm_block(B0 + 2, 2, 0)
                tb_low(B0 + 2, 0)
                q_low(B0 + 1, 1)
                norm_block(B0 + 3, 3, 1)
                tb_low(B0 + 3, 1)
                q_low(B0 + 2, 0)
                taps(B0, 0, 0, NTAP, False, first=True)
                norm_block(B0 + 4, 4, 0)
                tb_low(B0 + 4, 0)
                q_low(B0 + 3, 1)
                dw_low(B0)
                taps(B0 + 1, 1, 0, 4, False)
                mix(B0, 0)
                taps(B0 + 1, 1, 4, NTAP, False)
                t1_low(B0, 0)
                block_loop(dve, i, step_d)
                finish((i + 1) * BLOCKS - 1, STRIPS - 1, 1, True)
                if next_image:
                    next_stats(STRIPS - 2, 0)
                    next_stats(STRIPS - 1, 1).then_inc(gst_ready, 1)

            with dve.Fori(0, NIMG - 1) as i:
                image(i, True)
            image(NIMG - 1, False)

        @block.tensor
        def _(pe):
            mm = nc.tensor.matmul
            tr = nc.tensor.transpose
            pe.wait_ge(consts_loaded, 16 * NCONST)
            pe.wait_ge(consts_cast, 1)
            mm(bank[7][:, 0:1], wmat("wproj"), v("dwb"), start=True, stop=True).then_inc(cb_mm, 1)
            pe.wait_ge(weights_lo, 1)

            def group_norm(n):
                pe.wait_ge(gmv_ready, n + 1)
                mm(bank[7][:, 0:2], cmat("gmat"), mv[:], start=True, stop=True).then_inc(gmean_mm, 1)
                pe.wait_ge(gdev_ready, n + 1)
                mm(bank[7][:, 2:3], cmat("gmat"), gdev[:, 0:1], start=True, stop=True).then_inc(gvar_mm, 1)

            def ln_transpose(G, gg):
                pe.wait_ge(xg_ready, G + 1)
                for t in range(GROUP_PAIRS[gg]):
                    m = tr(bank[5][:, P * t:P * t + P], xg[:, gg, P * t:P * t + P], cmat("ident"))
                m.then_inc(xt_mm, 1)

            def ln_back(G, gg):
                pe.wait_ge(xc_ready, G + 1)
                for t in range(GROUP_PAIRS[gg]):
                    m = tr(bank[5][:, P * t:P * t + P], xc[:, gg, P * t:P * t + P], cmat("ident"))
                m.then_inc(xnt_mm, 1)

            def split_mm(out, w, x, start=True, stop=True):
                mm(out, w[0], x[0], start=start, stop=False)
                mm(out, w[1], x[0], start=False, stop=False)
                return mm(out, w[0], x[1], start=False, stop=stop)

            def project_k(G, gg):
                n = P * GROUP_PAIRS[gg]
                split_mm(bank[5][:, 0:n], [w[:, 1, :] for w in pws], [x[:, gg, 0:n] for x in xns])\
                    .then_inc(k_mm, 1)

            def project_q(G, gg):
                n = P * GROUP_PAIRS[gg]
                split_mm(bank[4][:, 0:n], [w[:, 0, :] for w in pws], [x[:, gg, 0:n] for x in xns])\
                    .then_inc(q_mm, 1)

            def project_v(G, gg):
                for t in range(GROUP_PAIRS[gg]):
                    c = slice(P * t, P * t + P)
                    m = mm(bank[4][:, c], xn[:, gg, c], wmat("wv"), start=True, stop=True)
                m.then_inc(v_mm, 1)

            def score_rows(G, gg, reuse):
                pe.wait_ge(q16_ready, G + 1)
                pe.wait_ge(k16_ready, G + 1)
                for w in range(2 * GROUP_PAIRS[gg]):
                    if reuse and w % 4 == 0:
                        pe.wait_ge(prob_ready, G * 2 - 1 + w // 4)
                    for jj in range(2):
                        c = 256 * (w % 2) + P * jj
                        m = mm(bank[w // 2][:, c:c + P],
                               q16[:, gg, w, 2 * jj:2 * jj + 2, :].rearrange("p j q -> p (j q)"),
                               k16[:, gg, w, :, :].rearrange("p s k -> p (s k)"), start=True, stop=True)
                m.then_inc(smax_mm, 1)

            def transpose_maxima(G, gg):
                pe.wait_ge(max_ready, G + 1)
                tr(bank[7][0:32, 448:512].bitcast(BF16), mx[:, gg, :], ident16[:]).then_inc(mt_mm, 1)

            def score_cols(G, gg, w0, w1, half_done):
                for w in range(w0, w1):
                    c = 256 * (w % 2)
                    for jj in range(2):
                        mm(bank[w // 2][:, c + P * jj:c + P * jj + P], sel16[:, 2 * w + jj, :], mt16[:, gg, :],
                           start=(jj == 0), stop=True, skip_group_check=True)
                    m = mm(bank[w // 2][:, c:c + 256], kx[:, gg, w, :, :].rearrange("p s k -> p (s k)"),
                           qbd[:, gg, w, :, :].rearrange("p j q -> p (j q)"), start=False, stop=True,
                           skip_group_check=True)
                if half_done:
                    m.then_inc(st_mm, 1)

            def attend(G, gg, h):
                for w in range(4 * h, min(4 * h + 4, 2 * GROUP_PAIRS[gg])):
                    t, w2 = w // 2, w % 2
                    for j in range(QUADS):
                        c = (t % 2) * QUADS * VCOLS + j * VCOLS
                        m = mm(bank[6 + h][64 * w2:64 * w2 + 64, c:c + VCOLS], prob[:, w, j, :],
                               vx[:, gg, w, j, :], start=True, stop=True)
                m.then_inc(pv_mm, 1)

            def out_transpose(G, gg):
                pe.wait_ge(oh_ready, G * 2 + 2)
                for t in range(GROUP_PAIRS[gg]):
                    m = tr(bank[4][:, P * t:P * t + P], oh[:, gg, P * t:P * t + P], cmat("ident"))
                m.then_inc(ot_mm, 1)

            def out_project(G, gg):
                n = P * GROUP_PAIRS[gg]
                pe.wait_ge(ot_ready, G + 1)
                mm(bank[5][:, 0:n], wmat("wout"), ot[:, gg, 0:n], start=True, stop=True).then_inc(out_mm, 1)

            def prologue(G):
                ln_transpose(G, 0)
                ln_back(G, 0)
                pe.wait_ge(xnl_ready, G + 1)
                project_k(G, 0)
                project_q(G, 0)
                pe.wait_ge(q_ready, G + 1)
                project_v(G, 0)
                ln_transpose(G + 1, 1)
                ln_back(G + 1, 1)

            def step(G, s, gg, near):
                ng = 1 - gg
                score_rows(G, gg, near(-1))
                if gg == 0 and near(1) and near(-1):
                    ln_back(G + 1, 1)
                if near(-2):
                    pe.wait_ge(v_ready, G + 1)
                    out_transpose(G - 2, gg)
                if near(-1):
                    pe.wait_ge(prob_ready, G * 2)
                    pe.wait_ge(v_ready, G)
                    attend(G - 1, ng, 0)
                if near(1):
                    pe.wait_ge(xn_ready, G + 2)
                if near(-2):
                    out_project(G - 2, gg)
                if near(-1):
                    attend(G - 1, ng, 1)
                transpose_maxima(G, gg)
                if near(1):
                    pe.wait_ge(xnl_ready, G + 2)
                    if not near(-2):
                        pe.wait_ge(v_ready, G + 1)
                    if gg == 0:
                        project_q(G + 1, ng)
                    if near(-2):
                        pe.wait_ge(ob_ready, G - 1)
                    project_k(G + 1, ng)
                    if gg == 1:
                        project_q(G + 1, ng)
                pe.wait_ge(mt_ready, G + 1)
                score_cols(G, gg, 0, 2, False)
                if near(2):
                    pe.wait_ge(k_ready, G + 2)
                    ln_transpose(G + 2, gg)
                score_cols(G, gg, 2, 4, True)
                score_cols(G, gg, 4, 2 * GROUP_PAIRS[gg], True)
                if near(1):
                    pe.wait_ge(q_ready, G + 2)
                    project_v(G + 1, ng)
                if gg == 0 and near(2):
                    ln_back(G + 2, 0)

            def epilogue(G0):
                G = G0 + GROUPS - 1
                out_transpose(G - 1, 0)
                pe.wait_ge(ob_ready, G - 1)
                out_project(G - 1, 0)
                pe.wait_ge(prob_ready, (G + 1) * 2)
                attend(G, 1, 0)
                attend(G, 1, 1)
                out_transpose(G, 1)
                pe.wait_ge(ob_ready, G)
                out_project(G, 1)

            with pe.Fori(0, NIMG) as i:
                group_norm(i * 2)
                group_loop(pe, i, step, prologue, epilogue)
                group_norm(i * 2 + 1)
                pe.wait_ge(ob_ready, (i + 1) * GROUPS)

                def lkv(s, sp, cc):
                    t0, n = KV_CHUNKS[cc]
                    for t in range(n):
                        c = slice(P * (t0 + t), P * (t0 + t) + P)
                        for k, (x, w) in enumerate(((tsth, lws[0]), (tsth, lws[1]), (tstl, lws[0]))):
                            if cc == 0 and t == 0 and k == 2:
                                pe.wait_ge(tstl_ready, i * STRIPS + s + 1)
                            m = mm(bank[2 + cc][:, 2 * P * t:2 * P * t + 2 * P], x[:, sp, c],
                                   w[:, 1:3, :].rearrange("p a b -> p (a b)"), start=(k == 0), stop=(k == 2))
                    m.then_inc(kv_mm, 1)

                def context(K, cc, first=False, last=False):
                    n = KV_CHUNKS[cc][1]
                    pe.wait_ge(krel_ready, K + 1)
                    for t in range(n):
                        m = mm(bank[6][:, 0:P], krel[:, cc, t, :], kv[:, cc, t, 1, :],
                               start=(first and t == 0), stop=(last and t == n - 1), skip_group_check=True)
                    m.then_inc(ctx_mm, 1)

                NK = len(KV_CHUNKS)

                def strip_c(s, sp, first):
                    pe.wait_ge(tsth_ready, i * STRIPS + s + 1)
                    for cc in range(NK):
                        lkv(s, sp, cc)
                        if cc >= CTX_LAG or not first:
                            context((i * STRIPS + s) * NK + cc - CTX_LAG, (cc - CTX_LAG) % NK,
                                    first=(first and cc == CTX_LAG))

                strip_c(0, 0, True)
                strip_c(1, 1, False)
                with pe.Fori(1, STRIPS // 2) as h:
                    for sp in range(2):
                        strip_c(h * 2 + sp, sp, False)
                for cc in range(NK - CTX_LAG, NK):
                    context((i + 1) * (STRIPS * NK) - NK + cc, cc, last=(cc == NK - 1))

                def lq(B, bb, n=4):
                    pe.wait_ge(tbh_ready, B + 1)
                    pe.wait_ge(tbl_ready, B + 1)
                    split_mm(bank[n][:, 0:BLOCK], [w[:, 0, :] for w in lws],
                             [tbh[:, bb, :], tbl[:, bb, :]]).then_inc(lq_mm, 1)

                def attention_out(B, bb, n=4):
                    pe.wait_ge(ql_ready, B + 1)
                    split_mm(bank[n][:, 0:BLOCK], [c[:] for c in ctxs], [qh[:, bb, :], ql[:, bb, :]])\
                        .then_inc(o_mm, 1)

                def project(B):
                    pe.wait_ge(dwl_ready, B + 1)
                    split_mm(bank[4][:, 0:BLOCK], [w[:, 3, :] for w in lws], [dwh[:], dwl[:]])\
                        .then_inc(proj_mm, 1)

                def fc1(B, bb, j):
                    if j >= FC1_BANKS:
                        pe.wait_ge(hf_ready, B * NF + j - FC1_BANKS + 1)
                    out = bank[j % FC1_BANKS][:, 0:BLOCK]
                    if j == 0:
                        pe.wait_ge(t1l_ready, B + 1)
                    split_mm(out, [x[:, P * j:P * j + P] for x in w1s], [t1h[:, bb, :], t1l[:, bb, :]])\
                        .then_inc(h_mm, 1)

                def fc2(B, bb, j):
                    out = bank[6 + bb][:, 0:BLOCK]
                    first, last = j == 0, j == NF - 1
                    if j in SPLIT_J:
                        k = SPLIT_J.index(j)
                        pe.wait_ge(hl_ready, B * NS + k + 1)
                        m = split_mm(out, [w[:, k, :] for w in w2s], [hh[:, k, :], hl[:, k, :]],
                                     start=first, stop=last)
                    else:
                        pe.wait_ge(hf_ready, B * NF + j + 1)
                        m = mm(out, w2[:, j, :], hw[:, WHOLE_J.index(j), :], start=first, stop=last)
                    if last:
                        m.then_inc(ff_mm, 1)

                def step_d(B, s, b, u, near):
                    bb = u % 2
                    for j in range(NF):
                        fc1(B, bb, j)
                        if j >= FC2_LAG:
                            fc2(B, bb, j - FC2_LAG)
                        if j == 1 and near(4):
                            pe.wait_ge(o_ready, B + 4)
                            lq(B + 4, bb)
                        if j == 5 and near(1):
                            if near(4):
                                pe.wait_ge(qh_ready, B + 5)
                            project(B + 1)
                    if near(4):
                        pe.wait_ge(t1_ready, B + 2)
                        attention_out(B + 4, bb)
                    for j in range(NF - FC2_LAG, NF):
                        fc2(B, bb, j)

                B0 = i * BLOCKS
                lq(B0, 0, n=0)
                lq(B0 + 1, 1, n=1)
                pe.wait_ge(ctxm_ready, i * 3 + 3)
                for k in range(4):
                    if k >= 2:
                        pe.wait_ge(o_ready, B0 + k - 1)
                    attention_out(B0 + k, k % 2, n=6 + k % 2)
                    if k < 2:
                        lq(B0 + k + 2, k % 2, n=k + 2)
                project(B0)
                block_loop(pe, i, step_d)


_HEAD_ORDER = np.concatenate([np.arange(HD) + HD * (j + 4 * s) for j in range(QUADS) for s in range(2)])


def _constants():
    eye = np.eye(P, dtype=np.float32)
    grp = np.arange(P) // (C // 32)
    gmat = (grp[:, None] == grp[None, :]).astype(np.float32) * np.float32(0.25)
    head = np.arange(P) // HD
    cmask = (head[:, None] == head[None, :]).astype(np.float32) * np.float32(HD ** -0.5)
    sel = np.zeros((32, 16, P), np.float32)
    for r in range(32):
        sel[r, r // 2, 64 * (r % 2):64 * (r % 2) + 64] = -1.0
    mask_lo = ((np.arange(P) // HD) % 2 == 0).astype(np.float32)
    return eye, gmat, cmask, sel, mask_lo, np.float32(1) - mask_lo


def kernel(**inputs):
    import concourse.bacc as _bacc
    from concourse.bass_utils import run_bass_kernel_spmd as _run

    a = {k: np.asarray(t) for k, t in inputs.items()}
    eye, gmat, cmask, sel, mask_lo, mask_hi = _constants()
    o = _HEAD_ORDER
    wqkv, bqkv = a["L0_conv_w_qkv"], a["L0_conv_b_qkv"]
    lw, lb = a["L1_conv_Wqkv"], a["L1_conv_bqkv"]
    col = {
        "gamma": a["L0_conv_ln_gamma"], "beta": a["L0_conv_ln_beta"], "bq": bqkv[0:C][o],
        "bk": bqkv[C:2 * C][o], "bout": a["L0_conv_b_out"], "dwb": a["L1_conv_dw_b"],
        "bproj": a["L1_conv_bproj"], "g1": a["L1_conv_bn1_g"], "b1": a["L1_conv_bn1_b"],
        "m1": a["L1_conv_bn1_m"], "v1": a["L1_conv_bn1_v"], "a1": np.broadcast_to(a["L1_conv_alpha1"], (C,)),
        "bfc2": a["L1_conv_bfc2"], "g2": a["L1_conv_bn2_g"], "b2": a["L1_conv_bn2_b"],
        "m2": a["L1_conv_bn2_m"], "v2": a["L1_conv_bn2_v"],
        "a2": np.broadcast_to(a["L1_conv_alpha2"], (C,)), "mask_lo": mask_lo, "mask_hi": mask_hi,
        "bv": bqkv[2 * C:][o], "blq": lb[0:C],
    }
    vec = np.stack([col[n] for n in VEC], axis=1)
    wmats = {
        "wq": wqkv[0:C][o].T, "wk": wqkv[C:2 * C][o].T, "wv": wqkv[2 * C:][o].T,
        "wout": a["L0_conv_w_out"][:, o].T, "lwq": lw[:, 0:C], "lwk": lw[:, C:2 * C],
        "lwv": lw[:, 2 * C:], "wproj": a["L1_conv_Wproj"],
    }
    cmats = {
        "ident": eye, "gmat": gmat, "cmask": cmask,
        "bias_lk": np.broadcast_to(lb[C:2 * C], (P, C)), "bias_lv": np.broadcast_to(lb[2 * C:], (P, C)),
    }
    arrays = {
        "x_in": a["x"].reshape(NIMG, C, HW),
        "vec_in": vec,
        "fc1b_in": a["L1_conv_bfc1"].reshape(NF, P).T,
        "dw_in": a["L1_conv_dw_w"].reshape(C, 9),
        "wm_in": np.stack([wmats[n] for n in WMATS], axis=1),
        "cm_in": np.stack([cmats[n] for n in CMATS], axis=1),
        "w1_in": a["L1_conv_Wfc1"],
        "w2_in": a["L1_conv_Wfc2"].reshape(NF, P, C).transpose(1, 0, 2),
        "sel_in": sel.reshape(32, 16 * P),
    }
    arrays = {k: np.ascontiguousarray(t) for k, t in arrays.items()}
    nc = _bacc.Bacc("TRN2", target_bir_lowering=False, num_devices=1)
    args = [nc.dram_tensor(k, t.shape, mybir.dt.from_np(t.dtype), kind="ExternalInput").ap()
            for k, t in arrays.items()]
    args.append(nc.dram_tensor("y_out", (NIMG, C, HW), F32, kind="ExternalOutput").ap())
    build(nc, *args)
    r = _run(nc, [arrays], core_ids=[0])
    return r.results[0]["y_out"].reshape(NIMG, C, H, W)
```
